# Optimizing a Trainium2 kernel written in Bass

```python
import numpy as np
import jax
import jax.numpy as jnp

def _softmax(x, axis=-1):
    return jax.nn.softmax(x, axis=axis)

def _gelu(x):
    return jax.nn.gelu(x, approximate=True)

def _silu(x):
    return jax.nn.silu(x)

def _sigmoid(x):
    return jax.nn.sigmoid(x)

def _layernorm(x, axis=-1, eps=1e-05):
    m = jnp.mean(x, axis=axis, keepdims=True)
    v = jnp.var(x, axis=axis, keepdims=True)
    return (x - m) / jnp.sqrt(v + eps)

def _scatter_add(tgt, idx, src, axis=0):
    return tgt.at[idx].add(src)

def _segment_sum(src, seg, n):
    return jax.ops.segment_sum(src, seg, n)
kernel_name = 'mk_adaln_d1_jaxref_r8_c5f8dd'

def setup_inputs(seed: int=0):
    np.random.seed(seed)
    _w = jnp.asarray

    def _L0_attn_setup():
        import jax, jax.numpy as jnp
        import numpy as np
        DECAY_MIN = 0.9
        DECAY_MAX = 0.999

        def _reference_tuple_inner(x, Wq, Wk, Wv, Wo, bo, Wg, bg, decay_param):
            B, L, D = x.shape
            M = Wq.shape[1]
            decay = DECAY_MIN + jax.nn.sigmoid(decay_param) * (DECAY_MAX - DECAY_MIN)
            q = x @ Wq
            k = x @ Wk
            v = x @ Wv
            gates = jax.nn.sigmoid(x @ Wg + bg)[..., 0]
            S0 = jnp.zeros((B, M, M), x.dtype)

            def scan_fn(S, inp):
                q_t, k_t, v_t, g_t = inp
                gk = k_t * g_t[:, None]
                gv = v_t * g_t[:, None]
                S = decay * S + gk[:, :, None] * gv[:, None, :]
                out_t = jnp.einsum('bd,bde->be', q_t, S)
                return (S, out_t)
            S_final, outs = jax.lax.scan(scan_fn, S0, (q.transpose(1, 0, 2), k.transpose(1, 0, 2), v.transpose(1, 0, 2), gates.T))
            outs = outs.transpose(1, 0, 2)
            y = outs @ Wo + bo
            return (y, S_final)
        key = jax.random.key(seed)
        ks = jax.random.split(key, 6)
        B, L, D, M = (8, 512, 128, 64)
        s = 0.02
        return {'x': jax.random.normal(ks[0], (B, L, D), jnp.float32), 'Wq': jax.random.normal(ks[1], (D, M), jnp.float32) * s, 'Wk': jax.random.normal(ks[2], (D, M), jnp.float32) * s, 'Wv': jax.random.normal(ks[3], (D, M), jnp.float32) * s, 'Wo': jax.random.normal(ks[4], (M, D), jnp.float32) * s, 'bo': jnp.zeros((D,), jnp.float32), 'Wg': jax.random.normal(ks[5], (D, 1), jnp.float32) * s, 'bg': jnp.zeros((1,), jnp.float32), 'decay_param': jnp.full((1,), 0.5, jnp.float32)}
    _L0_attn_in = _L0_attn_setup()

    def _L0_ffn_setup():
        import jax, jax.numpy as jnp
        import numpy as np
        B, S, H, F, E = (1, 256, 128, 256, 8)

        def _swiglu(x, wg, wu, wd):
            return jax.nn.silu(x @ wg.T) * (x @ wu.T) @ wd.T
        key = jax.random.key(seed)
        ks = jax.random.split(key, 8)
        sc = 1.0 / np.sqrt(H)
        scf = 1.0 / np.sqrt(F)
        return {'hidden_states': jax.random.normal(ks[0], (B, S, H), jnp.float32), 'gate_w': jax.random.normal(ks[1], (E, H), jnp.float32) * sc, 'shared_gate': jax.random.normal(ks[2], (F, H), jnp.float32) * sc, 'shared_up': jax.random.normal(ks[3], (F, H), jnp.float32) * sc, 'shared_down': jax.random.normal(ks[4], (H, F), jnp.float32) * scf, 'r_gate': jax.random.normal(ks[5], (E, F, H), jnp.float32) * sc, 'r_up': jax.random.normal(ks[6], (E, F, H), jnp.float32) * sc, 'r_down': jax.random.normal(ks[7], (E, H, F), jnp.float32) * scf}
    _L0_ffn_in = _L0_ffn_setup()
    _L0_c = _w((lambda *s: np.random.randn(*s).astype(np.float32) * 0.05)(8, 128))
    _L0_wmod = _w((lambda *s: np.random.randn(*s).astype(np.float32) * 0.05)(128, 6 * 128) * 128 ** (-0.5))
    _d = {'L0_attn_x': _L0_attn_in['x'], 'L0_attn_Wq': _L0_attn_in['Wq'], 'L0_attn_Wk': _L0_attn_in['Wk'], 'L0_attn_Wv': _L0_attn_in['Wv'], 'L0_attn_Wo': _L0_attn_in['Wo'], 'L0_attn_bo': _L0_attn_in['bo'], 'L0_attn_Wg': _L0_attn_in['Wg'], 'L0_attn_bg': _L0_attn_in['bg'], 'L0_attn_decay_param': _L0_attn_in['decay_param'], 'L0_ffn_gate_w': _L0_ffn_in['gate_w'], 'L0_ffn_shared_gate': _L0_ffn_in['shared_gate'], 'L0_ffn_shared_up': _L0_ffn_in['shared_up'], 'L0_ffn_shared_down': _L0_ffn_in['shared_down'], 'L0_ffn_r_gate': _L0_ffn_in['r_gate'], 'L0_ffn_r_up': _L0_ffn_in['r_up'], 'L0_ffn_r_down': _L0_ffn_in['r_down'], 'L0_c': _L0_c, 'L0_wmod': _L0_wmod}
    _x0 = _d['L0_attn_x']
    _d['L0_attn_x'] = jax.random.normal(jax.random.fold_in(jax.random.key(seed), 1), (8, 256, 128), dtype=_x0.dtype)
    del _x0
    return _d

def reference(L0_attn_x, L0_attn_Wq, L0_attn_Wk, L0_attn_Wv, L0_attn_Wo, L0_attn_bo, L0_attn_Wg, L0_attn_bg, L0_attn_decay_param, L0_ffn_gate_w, L0_ffn_shared_gate, L0_ffn_shared_up, L0_ffn_shared_down, L0_ffn_r_gate, L0_ffn_r_up, L0_ffn_r_down, L0_c, L0_wmod):

    def _L0_attn_ref(x, Wq, Wk, Wv, Wo, bo, Wg, bg, decay_param):
        import jax, jax.numpy as jnp
        import numpy as np
        DECAY_MIN = 0.9
        DECAY_MAX = 0.999

        def _reference_tuple_inner(x, Wq, Wk, Wv, Wo, bo, Wg, bg, decay_param):
            B, L, D = x.shape
            M = Wq.shape[1]
            decay = DECAY_MIN + jax.nn.sigmoid(decay_param) * (DECAY_MAX - DECAY_MIN)
            q = x @ Wq
            k = x @ Wk
            v = x @ Wv
            gates = jax.nn.sigmoid(x @ Wg + bg)[..., 0]
            S0 = jnp.zeros((B, M, M), x.dtype)

            def scan_fn(S, inp):
                q_t, k_t, v_t, g_t = inp
                gk = k_t * g_t[:, None]
                gv = v_t * g_t[:, None]
                S = decay * S + gk[:, :, None] * gv[:, None, :]
                out_t = jnp.einsum('bd,bde->be', q_t, S)
                return (S, out_t)
            S_final, outs = jax.lax.scan(scan_fn, S0, (q.transpose(1, 0, 2), k.transpose(1, 0, 2), v.transpose(1, 0, 2), gates.T))
            outs = outs.transpose(1, 0, 2)
            y = outs @ Wo + bo
            return (y, S_final)
        return _reference_tuple_inner(x, Wq, Wk, Wv, Wo, bo, Wg, bg, decay_param)[0]

    def _L0_ffn_ref(hidden_states, gate_w, shared_gate, shared_up, shared_down, r_gate, r_up, r_down):
        import jax, jax.numpy as jnp
        import numpy as np
        B, S, H, F, E = (1, 256, 128, 256, 8)

        def _swiglu(x, wg, wu, wd):
            return jax.nn.silu(x @ wg.T) * (x @ wu.T) @ wd.T
        b, s, h = hidden_states.shape
        x = hidden_states.reshape(-1, h)
        shared_out = _swiglu(x, shared_gate, shared_up, shared_down)
        logits = x @ gate_w.T
        top_id = jnp.argmax(logits, axis=-1)
        score = jax.nn.sigmoid(jnp.max(logits, axis=-1))
        xs = x * score[:, None]

        def body(acc, ws):
            wg, wu, wd, e = ws
            xe = jnp.where((top_id == e)[:, None], xs, 0.0)
            return (acc + _swiglu(xe, wg, wu, wd), None)
        acc0 = jnp.zeros_like(x)
        routed_out, _ = jax.lax.scan(body, acc0, (r_gate, r_up, r_down, jnp.arange(E)))
        return (shared_out + routed_out).reshape(b, s, h)
    x = L0_attn_x
    mod = (_silu(L0_c) @ L0_wmod).reshape(L0_c.shape[0], 6, 1, -1)
    sa, ca, ga, sb, cb, gb = (mod[:, 0], mod[:, 1], mod[:, 2], mod[:, 3], mod[:, 4], mod[:, 5])
    ga = (2 * (ga >= 0) - 1) * jnp.maximum(jnp.abs(ga), 0.25)
    gb = (2 * (gb >= 0) - 1) * jnp.maximum(jnp.abs(gb), 0.25)
    h = _layernorm(x, axis=-1) * (1 + ca) + sa
    x = x + ga * _L0_attn_ref(h, L0_attn_Wq, L0_attn_Wk, L0_attn_Wv, L0_attn_Wo, L0_attn_bo, L0_attn_Wg, L0_attn_bg, L0_attn_decay_param)
    h = _layernorm(x, axis=-1) * (1 + cb) + sb
    x = x + gb * _L0_ffn_ref(h, L0_ffn_gate_w, L0_ffn_shared_gate, L0_ffn_shared_up, L0_ffn_shared_down, L0_ffn_r_gate, L0_ffn_r_up, L0_ffn_r_down)
    return x

_drawn_inputs = setup_inputs


def setup_inputs(seed=0):
    import zlib

    import numpy as np

    out = dict(_drawn_inputs(seed))
    spreads = {'L0_attn_bo': (0.0, 2.0)}
    factors = {'L0_attn_Wq': 8.0,
     'L0_attn_Wk': 8.0,
     'L0_attn_Wv': 7.992,
     'L0_attn_Wo': 7.869,
     'L0_attn_Wg': 8.0,
     'L0_ffn_gate_w': 8.0,
     'L0_ffn_shared_gate': 8.0,
     'L0_ffn_shared_up': 8.0,
     'L0_ffn_shared_down': 8.0,
     'L0_ffn_r_gate': 8.0,
     'L0_ffn_r_up': 8.0,
     'L0_ffn_r_down': 8.0}
    for name, (base, spread) in spreads.items():
        noise = np.random.default_rng([zlib.crc32(name.encode()), seed]).standard_normal(out[name].shape)
        drawn = base * np.exp(spread * noise) if base else spread * noise
        out[name] = jnp.asarray(drawn.astype(out[name].dtype))
    for name, factor in factors.items():
        out[name] = (out[name] * factor).astype(out[name].dtype)
    return out
```

```python
from contextlib import ExitStack

import concourse.bass as bass
from concourse import mybir

F32 = mybir.dt.float32
BF16 = mybir.dt.bfloat16
I32 = mybir.dt.int32
ACT = mybir.ActivationFunctionType
ALU = mybir.AluOpType
AX_X = mybir.AxisListType.X

P = 128
B, L, D = 8, 256, 128
M = 64
F, E = 256, 8
FB = F // P
TPB = L // P
NT = B * TPB
NR = NT + E - 1
ROW = 2 * D + 1
G, TG = 4, NT // 4
BG = B // G
RING = 4
OG = -(-(NR + 4) // RING)
EPS = 1e-5
DECAY_MIN, DECAY_MAX = 0.9, 0.999
NO_TOKEN = 1 << 20
ds = bass.ds


def adaln_block(nc, x, proj, row, modin, w_gu, w_down, out):
    sorted_rows = nc.dram_tensor("sorted_rows", (NR * P, ROW), F32).ap()

    with ExitStack() as ctx:
        def sb(name, shape, dt=F32):
            return ctx.enter_context(nc.sbuf_tensor(name, shape, dt))

        def sem(name):
            return ctx.enter_context(nc.semaphore(name))

        bank = [ctx.enter_context(nc.psum_tensor(f"bank{i}", [P, 512], F32)) for i in range(8)]

        x_all = sb("x_all", [P, NT, D])
        projs = sb("projs", [M, 4 * D])
        rowb = sb("rowb", [P, D + 2])
        mods = sb("mods", [P, 8 + 6 * D + 1 + E])
        wgu = sb("wgu", [P, (E + 1) * 2 * F])
        wdn = sb("wdn", [P, (E + 1) * FB * D])
        c_t = mods[:, 0:8]
        wmod = mods[:, 8:8 + 6 * D]
        wg_col = mods[:, 8 + 6 * D:9 + 6 * D]
        gate_w = mods[:, 9 + 6 * D:9 + 6 * D + E]

        onef = sb("onef", [P, 2 * P])
        ident = sb("ident", [P, 2 * P])
        upto_self = sb("upto_self", [P, P], BF16)
        oneb = sb("oneb", [P, P], BF16)
        rev_i = sb("rev_i", [P, NT, E], I32)
        rev = sb("rev", [P, NT, E])
        tile_i = sb("tile_i", [P, NR, E - 1], I32)
        tile_f = sb("tile_f", [P, NR, E - 1])
        first0 = sb("first0", [P, E * NT])
        mhalf = sb("mhalf", [P, NT])
        eps = sb("eps", [P, TPB])
        pad_row = sb("pad_row", [P, ROW])

        sigs = sb("sigs", [P, 9])
        warm = sb("warm", [P, 1])
        siluc = sb("siluc", [P, 8])
        decay = sb("decay", [P, 1])
        decay_pow = sb("decay_pow", [P, 3 * P])
        shsc = sb("shsc", [P, 4, B])
        gneg = sb("gneg", [B, 2 * D])
        gabs = sb("gabs", [B, 2 * D])
        gsign = sb("gsign", [B, 2 * D])
        grow = sb("grow", [B, 2 * D])
        gab = sb("gab", [P, B, 2 * D])
        gabo = sb("gabo", [P, B, D])
        a_sb = sb("a_sb", [P, D])
        wvo = sb("wvo", [P, D])
        wvog = sb("wvog", [P, B * (D + 2)])
        st1 = sb("st1", [P, NT, 6])
        mv1 = sb("mv1", [P, NT, 2])
        ve1 = sb("ve1", [P, NT])
        rstd1 = sb("rstd1", [P, NT])

        xn1 = [sb(f"xn1_{s}", [P, L]) for s in range(2)]
        h_t = [sb(f"h_t{s}", [P, L]) for s in range(2)]
        q_t = [sb(f"q_t{s}", [P, L]) for s in range(2)]
        gate = [sb(f"gate{s}", [P, TPB]) for s in range(2)]
        gate2 = [sb(f"gate2_{s}", [P, TPB]) for s in range(2)]
        vo = [sb(f"vo{s}", [P, L]) for s in range(2)]
        p_t = [sb(f"p_t{s}", [P, 3 * P]) for s in range(2)]
        st2 = [sb(f"st2_{s}", [P, TPB, 6]) for s in range(2)]
        mv2 = [sb(f"mv2_{s}", [P, TPB, 2]) for s in range(2)]
        ve2 = [sb(f"ve2_{s}", [P, TPB]) for s in range(2)]
        rstd2 = [sb(f"rstd2_{s}", [P, TPB]) for s in range(2)]
        xn2 = [sb(f"xn2_{s}", [P, L]) for s in range(2)]
        score = [sb(f"score{s}", [P, TPB]) for s in range(2)]
        xb = sb("xb", [P, B * L])
        x1 = sb("x1", [P, NT, D])
        h2_all = sb("h2_all", [P, B * L])
        pay = sb("pay", [P, NT, ROW])

        top = sb("top", [P, NT])
        eq = sb("eq", [P, NT, E])
        cand = sb("cand", [P, NT, E])
        best = sb("best", [P, NT])
        one_hot = sb("one_hot", [P, E, NT], BF16)
        upto = sb("upto", [P, E, NT])
        padded_cnt = sb("padded_cnt", [P, E])
        ends = sb("ends", [P, E])
        base = sb("base", [P, E])
        place = sb("place", [P, E, NT])
        pos = sb("pos", [P, NT], I32)
        past = sb("past", [P, NR, E - 1])
        expert = sb("expert", [P, OG * RING + 3])
        offsets = sb("offsets", [P, OG, 2, RING], I32)

        sg = [sb(f"sg{f}", [P, 512]) for f in range(FB)]
        acts = [sb(f"acts{s}", [P, FB * 512]) for s in range(2)]
        shg = [sb(f"shg{s}", [P, 512]) for s in range(2)]

        rows = [sb(f"rows{k}", [P, D]) for k in range(RING)]
        meta = sb("meta", [P, NR, ROW - D])
        token = [sb(f"token{k}", [P, 1], I32) for k in range(RING)]
        xs_t = [sb(f"xs_t{s}", [P, P]) for s in range(2)]
        sge = [sb(f"sge{s}", [P, F]) for s in range(2)]
        acte = [sb(f"acte{s}", [P, F]) for s in range(2)]
        act_t = [sb(f"act_t{s}", [P, F]) for s in range(2)]
        y = [sb(f"y{k}", [P, D]) for k in range(RING)]

        row_in, mod_in, proj_in = sem("row_in"), sem("mod_in"), sem("proj_in")
        x_in = [sem(f"x_in{i}") for i in range(4)]
        shared_in, routed_in = sem("shared_in"), sem("routed_in")
        padded, scattered, meta_in = sem("padded"), sem("scattered"), sem("meta_in")
        base_out = sem("base_out")
        rows_in = [sem(f"rows_in{k}") for k in range(RING)]
        added = [sem(f"added{k}") for k in range(RING)]
        const_step, const_ready = sem("const_step"), sem("const_ready")
        sig_ready, setup_step = sem("sig_ready"), sem("setup_step")
        silu_ready, mod_done, mod_ready = sem("silu_ready"), sem("mod_done"), sem("mod_ready")
        merge_done, merge_ready = sem("merge_done"), sem("merge_ready")
        grow_ready, gab_done, gab_ready = sem("grow_ready"), sem("gab_done"), sem("gab_ready")
        wg_ready, wvog_ready, gabo_ready = sem("wg_ready"), sem("wvog_ready"), sem("gabo_ready")
        decay_ready = sem("decay_ready")
        stat1_ready, ve1_ready, rstd1_ready = sem("stat1_ready"), sem("ve1_ready"), sem("rstd1_ready")
        xn1_ready, t1_done, h_ready = sem("xn1_ready"), sem("t1_done"), sem("h_ready")
        q_done, q_ready, vo_done, vo_ready = sem("q_done"), sem("q_ready"), sem("vo_done"), sem("vo_ready")
        gate_step, gate2_step = sem("gate_step"), sem("gate2_step")
        s_done, p_ready, y_done = sem("s_done"), sem("p_ready"), sem("y_done")
        xb_ready, x1_ready, st2_step = sem("xb_ready"), sem("x1_ready"), sem("st2_step")
        mv2_ready, ve2_step, rstd2_ready = sem("mv2_ready"), sem("ve2_step"), sem("rstd2_ready")
        xn2_ready, t2_done, h2_ready = sem("xn2_ready"), sem("t2_done"), sem("h2_ready")
        logit_done, top_ready, score_ready = sem("logit_done"), sem("top_ready"), sem("score_ready")
        t3_done, xs_ready, gb_in = sem("t3_done"), sem("xs_ready"), sem("gb_in")
        route_step, hot_ready, rank_done = sem("route_step"), sem("hot_ready"), sem("rank_done")
        pos_ready, expert_ready = sem("pos_ready"), sem("expert_ready")
        shgu_done, shsilu_ready, shact_ready = sem("shgu_done"), sem("shsilu_ready"), sem("shact_ready")
        shdown_done, shg_ready, base_ready = sem("shdown_done"), sem("shg_ready"), sem("base_ready")
        xr_done, xs_t_ready, gu_done = sem("xr_done"), sem("xs_t_ready"), sem("gu_done")
        silu_e_ready, act_ready, actt_done = sem("silu_e_ready"), sem("act_ready"), sem("actt_done")
        act_t_ready, down_done, y_ready = sem("act_t_ready"), sem("down_done"), sem("y_ready")
        token_ready = sem("token_ready")

        block = ctx.enter_context(nc.Block())

        x_tiles = x.rearrange("b (t p) d -> p (b t) d", p=P)
        out_tiles = out.rearrange("b (t p) d -> p (b t) d", p=P)
        out_rows = out.rearrange("b l d -> (b l) d")
        sorted_tiles = sorted_rows.rearrange("(j p) c -> p j c", p=P)
        SH = E * 2 * F
        SHD = E * FB * D

        @block.sync
        def _(sp):
            sp.dma_start(mods[:], modin).then_inc(mod_in, 16)
            for i in range(4):
                sp.dma_start(x_all[:, 4 * i:4 * i + 4, :], x_tiles[:, 4 * i:4 * i + 4, :]).then_inc(x_in[i], 16)
            sp.dma_start(wgu[:, SH:], w_gu[:, SH:]).then_inc(shared_in, 16)
            sp.dma_start(wdn[:, SHD:], w_down[:, SHD:]).then_inc(shared_in, 16)
            sp.wait_ge(const_ready, 1)
            sp.dma_start(sorted_tiles, pad_row[:].unsqueeze(1).to_broadcast([P, NR, ROW])).then_inc(padded, 16)
            sp.dma_start(wgu[:, 0:SH], w_gu[:, 0:SH]).then_inc(routed_in, 16)
            sp.dma_start(wdn[:, 0:SHD], w_down[:, 0:SHD]).then_inc(routed_in, 16)
            sp.wait_ge(gab_ready, B // 2)
            for t in range(TPB):
                sp.dma_start(pay[:, t:NT:TPB, D:2 * D], gab[:, :, D:2 * D]).then_inc(gb_in, 16)
            def base(g):
                sp.wait_ge(base_ready, g + 1)
                sp.dma_start(out_tiles[:, g * TG:(g + 1) * TG, :], x1[:, g * TG:(g + 1) * TG, :]).then_inc(base_out, 16)

            base(0)
            base(1)
            sp.wait_ge(scattered, 16 * NT)

            def load_rows(j, k, first):
                if not first:
                    sp.wait_ge(xr_done, j - RING + 1)
                sp.dma_start(rows[k][:], sorted_rows[ds(j * P, P), 0:D]).then_inc(rows_in[k], 16)

            for j in range(RING):
                load_rows(j, j, True)
            for lo, hi in ((0, RING), (RING, NR)):
                sp.dma_start(meta[:, lo:hi, :], sorted_tiles[:, lo:hi, D:ROW]).then_inc(meta_in, 16)
                if lo == 0:
                    base(2)
                    base(3)
            with sp.Fori(1, NR // RING) as i:
                for k in range(RING):
                    load_rows(i * RING + k, k, False)
            for j in range(NR // RING * RING, NR):
                load_rows(j, j % RING, False)
            sp.wait_ge(base_out, 16 * G)
            for k in range(RING):
                sp.wait_ge(added[k], 16 * ((NR - 1 - k) // RING + 1))

        @block.gpsimd
        def _(pool):
            nc.gpsimd.memset(onef[:], 1.0).then_inc(const_step, 1)
            pool.wait_ge(const_step, 1)
            nc.gpsimd.affine_select(out=ident[:], in_=onef[:], compare_op=ALU.is_equal, fill=0.0, base=0,
                                    pattern=[[-1, 2 * P]], channel_multiplier=1)
            nc.gpsimd.memset(mhalf[:], -0.5)
            nc.gpsimd.memset(eps[:], EPS)
            nc.gpsimd.memset(pad_row[:, 0:2 * D], 0.0)
            nc.gpsimd.memset(pad_row[:, 2 * D:ROW].bitcast(I32), NO_TOKEN).then_inc(const_ready, 1)
            def rstd_first(part, lo, hi):
                pool.wait_ge(stat1_ready, part + 1)
                nc.gpsimd.tensor_scalar(ve1[:, lo:hi], mv1[:, lo:hi, 1], EPS, None, ALU.add).then_inc(ve1_ready, 1)
                pool.wait_ge(ve1_ready, part + 1)
                nc.gpsimd.tensor_tensor(rstd1[:, lo:hi], ve1[:, lo:hi], mhalf[:, lo:hi], ALU.pow).then_inc(rstd1_ready, 1)

            wv = wvog[:].rearrange("p (b n) -> p b n", b=B)

            def weights(b):
                pool.wait_ge(gab_ready, b // 2 + 1)
                nc.gpsimd.tensor_tensor(wv[:, b, 0:D], gab[:, b, 0:D], wvo[:], ALU.mult).then_inc(wvog_ready, 1)

            def residual(b):
                nc.gpsimd.tensor_tensor(gabo[:, b, :], gab[:, b, 0:D], rowb[:, 0:D], ALU.mult).then_inc(gabo_ready, 1)
                pool.wait_ge(gabo_ready, b + 1)
                nc.gpsimd.tensor_tensor(
                    xb[:, b * L:(b + 1) * L].rearrange("p (t d) -> p t d", t=TPB), x_all[:, b * TPB:(b + 1) * TPB, :],
                    gabo[:, b:b + 1, :].to_broadcast([P, TPB, D]), ALU.add).then_inc(xb_ready, 1)

            def rstd(b):
                s = b % 2
                pool.wait_ge(mv2_ready, b + 1)
                nc.gpsimd.tensor_tensor(ve2[s][:], mv2[s][:, :, 1], eps[:, 0:TPB], ALU.add).then_inc(ve2_step, 1)
                pool.wait_ge(ve2_step, b + 1)
                nc.gpsimd.tensor_tensor(rstd2[s][:], ve2[s][:], mhalf[:, 0:TPB], ALU.pow).then_inc(rstd2_ready, 1)

            rstd_first(0, 0, 4)
            pool.wait_ge(mod_in, 16)
            nc.gpsimd.tensor_copy(wv[:, :, D], wg_col.to_broadcast([P, B])).then_inc(wg_ready, 1)
            pool.wait_ge(merge_ready, 1)
            weights(0)
            weights(1)
            rstd_first(1, 4, NT)
            pool.wait_ge(row_in, 16)
            for i in range(4):
                pool.wait_ge(x_in[i], 16)
            residual(0)
            weights(2)
            residual(1)
            nc.gpsimd.memset(oneb[:], 1.0).then_inc(const_step, 1)
            nc.gpsimd.memset(upto_self[:], -1.0).then_inc(const_step, 1)
            pool.wait_ge(const_step, 3)
            nc.gpsimd.affine_select(out=upto_self[:], in_=upto_self[:], compare_op=ALU.is_ge, fill=0.0, base=0,
                                    pattern=[[-1, P]], channel_multiplier=1)
            nc.gpsimd.iota(rev_i[:], pattern=[[0, NT], [-1, E]], base=E, channel_multiplier=0)
            nc.gpsimd.iota(tile_i[:], pattern=[[P, NR], [0, E - 1]], base=0, channel_multiplier=0)
            nc.gpsimd.memset(first0[:], 1.0)
            nc.gpsimd.iota(pay[:, :, 2 * D:ROW].bitcast(I32), pattern=[[P, NT]], base=0,
                           channel_multiplier=1).then_inc(const_step, 1)
            rstd(0)
            pool.wait_ge(const_step, 4)
            nc.gpsimd.tensor_copy(rev[:], rev_i[:])
            nc.gpsimd.tensor_copy(tile_f[:], tile_i[:])
            nc.gpsimd.memset(first0[:, 0:E * NT:NT], 0.0)
            nc.gpsimd.memset(expert[:], 0.0).then_inc(const_ready, 1)
            for b in range(1, B):
                if b + 2 < B:
                    weights(b + 2)
                if b + 1 < B:
                    residual(b + 1)
                rstd(b)
            pool.wait_ge(padded, 16)
            pool.wait_ge(pos_ready, 1)
            pool.wait_ge(xs_ready, B)
            pool.wait_ge(gb_in, 16 * TPB)
            for t in range(NT):
                nc.gpsimd.indirect_dma_start(sorted_rows, bass.IndirectOffsetOnAxis(pos[:, t:t + 1], 0),
                                             pay[:, t, :], None).then_inc(scattered, 16)
            pool.wait_ge(base_out, 16 * G)
            pool.wait_ge(meta_in, 32)

            def add_rows(j, k, wave):
                if wave is not None:
                    pool.wait_ge(added[k], 16 * wave)
                pool.wait_ge(y_ready, j + 1)
                nc.gpsimd.tensor_copy(token[k][:], meta[:, ds(j, 1), D:D + 1].bitcast(I32).rearrange(
                    "p a c -> p (a c)")).then_inc(token_ready, 1)
                pool.wait_ge(base_out, 16 * G)
                pool.wait_ge(token_ready, j + 1)
                nc.gpsimd.indirect_dma_start(out_rows, bass.IndirectOffsetOnAxis(token[k][:], 0), y[k][:], None,
                                             bounds_check=B * L - 1, oob_is_err=False,
                                             compute_op=ALU.add).then_inc(added[k], 16)

            for j in range(RING):
                add_rows(j, j, None)
            with pool.Fori(1, NR // RING) as i:
                for k in range(RING):
                    add_rows(i * RING + k, k, i)
            for j in range(NR // RING * RING, NR):
                add_rows(j, j % RING, j // RING)

        @block.scalar
        def _(act):
            act.dma_start(rowb[:], row.partition_broadcast(P)).then_inc(row_in, 16)
            act.dma_start(projs[:], proj).then_inc(proj_in, 16)
            act.wait_ge(const_ready, 1)
            nc.scalar.activation(warm[:], mhalf[:, 0:1], ACT.Sigmoid)
            act.wait_ge(mod_in, 16)
            nc.scalar.activation(sigs[:, 0:8], c_t, ACT.Sigmoid).then_inc(sig_ready, 1)
            act.wait_ge(row_in, 16)
            nc.scalar.activation(sigs[:, 8:9], rowb[:, D + 1:D + 2], ACT.Sigmoid).then_inc(sig_ready, 1)
            act.wait_ge(merge_done, 1)
            nc.scalar.copy(a_sb[:], bank[0][:, 0:D])
            nc.scalar.copy(wvo[:], bank[0][:, D:2 * D]).then_inc(merge_ready, 1)

            def gates_out(i):
                act.wait_ge(gab_done, i + 1)
                nc.scalar.copy(gab[:, 2 * i:2 * i + 2, :].rearrange("p b d -> p (b d)"), bank[4 + i][:]).then_inc(gab_ready, 1)

            def h_out(b):
                act.wait_ge(t1_done, b + 1)
                if b >= 2:
                    act.wait_ge(s_done, b - 1)
                    act.wait_ge(vo_done, b - 1)
                nc.scalar.activation(h_t[b % 2][:], bank[0][:, 0:L], ACT.Identity, bias=shsc[:, 0, b:b + 1],
                                     scale=shsc[:, 1, b:b + 1]).then_inc(h_ready, 1)

            def h2_out(b):
                act.wait_ge(t2_done, b + 1)
                nc.scalar.activation(h2_all[:, b * L:(b + 1) * L], bank[5][:, 0:L], ACT.Identity,
                                     bias=shsc[:, 2, b:b + 1], scale=shsc[:, 3, b:b + 1]).then_inc(h2_ready, 1)

            def gate_out(b):
                act.wait_ge(vo_done, b + 1)
                nc.scalar.activation(gate[b % 2][:], bank[2][:].rearrange("p (t n) -> p t n", t=TPB)[:, :, D],
                                     ACT.Sigmoid, bias=rowb[:, D:D + 1]).then_inc(gate_step, 1)

            def q_out(b):
                act.wait_ge(q_done, b + 1)
                nc.scalar.copy(q_t[b % 2][:], bank[1][:, 0:L]).then_inc(q_ready, 1)

            def gate2_out(b):
                act.wait_ge(gate_step, b + 1)
                nc.scalar.activation(gate2[b % 2][:], gate[b % 2][:], ACT.Square).then_inc(gate2_step, 1)

            def score_out(b):
                act.wait_ge(top_ready, b + 1)
                nc.scalar.activation(score[b % 2][:], top[:, b * TPB:(b + 1) * TPB], ACT.Sigmoid).then_inc(score_ready, 1)

            def vo_out(b):
                s = b % 2
                act.wait_ge(gate2_step, b + 1)
                if b >= 2:
                    act.wait_ge(y_done, b - 1)
                for t in range(TPB):
                    last = nc.scalar.mul(vo[s][:, t * D:(t + 1) * D], bank[2][:, t * 256:t * 256 + D],
                                         gate2[s][:, t:t + 1])
                last.then_inc(vo_ready, 1)

            def xs_out(b):
                act.wait_ge(score_ready, b + 1)
                act.wait_ge(t3_done, b + 1)
                for t in range(TPB):
                    last = nc.scalar.mul(pay[:, b * TPB + t, 0:D], bank[7][:, t * D:(t + 1) * D],
                                         score[b % 2][:, t:t + 1])
                last.then_inc(xs_ready, 1)

            act.wait_ge(mod_ready, 1)
            for b in range(B + 3):
                if b < B:
                    h_out(b)
                if b == 0:
                    gates_out(0)
                if b >= 3:
                    h2_out(b - 3)
                if b < B:
                    gate_out(b)
                    q_out(b)
                    gate2_out(b)
                if b == 0:
                    gates_out(1)
                if b >= 3:
                    score_out(b - 3)
                if b < B:
                    vo_out(b)
                if b >= 3:
                    xs_out(b - 3)

            def shared_silu(g, f):
                act.wait_ge(shgu_done, g * FB + (f + 1))
                if f > 0 or not isinstance(g, int):
                    act.wait_ge(shact_ready, g * FB + f - 1)
                nc.scalar.activation(sg[f][:], bank[2 * f][:], ACT.Silu).then_inc(shsilu_ready, 1)

            for f in range(FB):
                shared_silu(0, f)
            with act.Fori(1, G) as g:
                for f in range(FB):
                    shared_silu(g, f)

            def xs_t_out(j, s, early):
                act.wait_ge(xr_done, j + 1)
                if not early:
                    act.wait_ge(gu_done, j - 1)
                nc.scalar.copy(xs_t[s][:], bank[6][:, 0:P]).then_inc(xs_t_ready, 1)

            def silu_out(j, s, early):
                act.wait_ge(gu_done, j + 1)
                if not early:
                    act.wait_ge(act_ready, j - 1)
                nc.scalar.activation(sge[s][:], bank[s][:, 0:F], ACT.Silu).then_inc(silu_e_ready, 1)

            xs_t_out(0, 0, True)
            for j in range(2):
                xs_t_out(j + 1, (j + 1) % 2, j == 0)
                silu_out(j, j, True)
            with act.Fori(0, (NR - 3) // RING) as i:
                for k in range(RING):
                    j = i * RING + (2 + k)
                    xs_t_out(j + 1, (k + 1) % 2, False)
                    silu_out(j, k % 2, False)
            silu_out(NR - 1, (NR - 1) % 2, False)

        @block.vector
        def _(dve):
            steps = [0]

            def chain(ins, signal=setup_step):
                steps[0] += 1
                ins.then_inc(signal, 1)
                dve.wait_ge(signal, steps[0])

            def stats1(lo, hi):
                for t in range(lo, hi):
                    if t % 4 == 0:
                        dve.wait_ge(x_in[t // 4], 16)
                    last = nc.vector.bn_stats(st1[:, t, :], x_all[:, t, :])
                chain(last)
                for t in range(lo, hi):
                    last = nc.vector.bn_aggr(mv1[:, t, :], st1[:, t, :])
                last.then_inc(stat1_ready, 1)

            logits = bank[6][:, 0:NT * E].rearrange("p (t e) -> p t e", t=NT)

            def choose(lo, hi):
                n = hi - lo
                if lo == 0:
                    dve.wait_ge(const_ready, 2)
                dve.wait_ge(top_ready, hi // TPB)
                chain(nc.vector.tensor_tensor(eq[:, lo:hi, :], logits[:, lo:hi, :],
                                              top[:, lo:hi].unsqueeze(2).to_broadcast([P, n, E]), ALU.is_equal))
                chain(nc.vector.tensor_tensor(cand[:, lo:hi, :], eq[:, lo:hi, :], rev[:, lo:hi, :], ALU.mult))
                chain(nc.vector.tensor_reduce(best[:, lo:hi], cand[:, lo:hi, :], AX_X, ALU.max))
                nc.vector.tensor_tensor(one_hot[:, :, lo:hi].rearrange("p e t -> p t e"), cand[:, lo:hi, :],
                                        best[:, lo:hi].unsqueeze(2).to_broadcast([P, n, E]),
                                        ALU.is_equal).then_inc(hot_ready, 1)

            dve.wait_ge(sig_ready, 1)
            nc.vector.tensor_tensor(siluc[:], sigs[:, 0:8], c_t, ALU.mult).then_inc(silu_ready, 1)
            stats1(0, 4)
            dve.wait_ge(mod_done, 1)
            mod_t = bank[1][:, 0:4 * B].rearrange("p (k b) -> p k b", k=4)
            nc.vector.tensor_copy(shsc[:, 0:4:2, :], mod_t[:, 0:4:2, :])
            nc.vector.tensor_scalar(shsc[:, 1:4:2, :], mod_t[:, 1:4:2, :], 1.0, None, ALU.add).then_inc(mod_ready, 1)
            dve.wait_ge(mod_done, 2)
            graw = bank[2][0:B, 0:2 * D]
            nc.vector.tensor_scalar(gsign[:], graw, 0.0, 0.5, ALU.is_ge, ALU.subtract)
            chain(nc.vector.tensor_scalar(gneg[:], graw, -2.0, None, ALU.mult))
            chain(nc.vector.scalar_tensor_tensor(out=gabs[:], in0=graw, scalar=2.0, in1=gneg[:], op0=ALU.mult,
                                                 op1=ALU.max))
            nc.vector.scalar_tensor_tensor(out=grow[:], in0=gabs[:], scalar=0.5, in1=gsign[:], op0=ALU.max,
                                           op1=ALU.mult).then_inc(grow_ready, 1)

            def norm1(b):
                s = b % 2
                dve.wait_ge(rstd1_ready, 1 if b < 2 else 2)
                if b >= 2:
                    dve.wait_ge(t1_done, b - 1)
                for t in range(TPB):
                    g = b * TPB + t
                    last = nc.vector.tensor_scalar(xn1[s][:, t * D:(t + 1) * D], x_all[:, g, :], mv1[:, g, 0:1],
                                                   rstd1[:, g:g + 1], ALU.subtract, ALU.mult)
                last.then_inc(xn1_ready, 1)

            def norm2(b):
                s = b % 2
                dve.wait_ge(rstd2_ready, b + 1)
                if b >= 2:
                    dve.wait_ge(t2_done, b - 1)
                for t in range(TPB):
                    last = nc.vector.tensor_scalar(xn2[s][:, t * D:(t + 1) * D], x1[:, b * TPB + t, :],
                                                   mv2[s][:, t, 0:1], rstd2[s][:, t:t + 1], ALU.subtract, ALU.mult)
                last.then_inc(xn2_ready, 1)

            def masked(b):
                dve.wait_ge(s_done, b + 1)
                if b >= 2:
                    dve.wait_ge(y_done, b - 1)
                nc.vector.tensor_tensor(p_t[b % 2][:], bank[3][:, 0:3 * P], decay_pow[:], ALU.mult).then_inc(p_ready, 1)

            def top_logit(b):
                dve.wait_ge(logit_done, b + 1)
                nc.vector.tensor_reduce(top[:, b * TPB:(b + 1) * TPB], bank[6][:, b * TPB * E:(b + 1) * TPB * E].rearrange(
                    "p (t e) -> p t e", t=TPB), AX_X, ALU.max).then_inc(top_ready, 1)

            def attended(b):
                s = b % 2
                dve.wait_ge(y_done, b + 1)
                dve.wait_ge(xb_ready, b + 1)
                nc.vector.tensor_tensor(x1[:, b * TPB:(b + 1) * TPB, :], bank[4][:, 0:L].rearrange("p (t d) -> p t d", t=TPB),
                                        xb[:, b * L:(b + 1) * L].rearrange("p (t d) -> p t d", t=TPB), ALU.add
                                        ).then_inc(x1_ready, 1)

            def stats2(b):
                s = b % 2
                dve.wait_ge(x1_ready, b + 1)
                for t in range(TPB):
                    last = nc.vector.bn_stats(st2[s][:, t, :], x1[:, b * TPB + t, :])
                last.then_inc(st2_step, 1)

            def moments2(b):
                s = b % 2
                dve.wait_ge(st2_step, b + 1)
                for t in range(TPB):
                    last = nc.vector.bn_aggr(mv2[s][:, t, :], st2[s][:, t, :])
                last.then_inc(mv2_ready, 1)

            norm1(0)
            norm1(1)
            dve.wait_ge(sig_ready, 2)
            chain(nc.vector.tensor_scalar(decay[:], sigs[:, 8:9], DECAY_MAX - DECAY_MIN, DECAY_MIN, ALU.mult, ALU.add))
            dve.wait_ge(const_ready, 1)
            chain(nc.vector.tensor_tensor_scan(decay_pow[:, 0:2 * P], decay[:].to_broadcast([P, 2 * P]), ident[:], 0.0,
                                               ALU.mult, ALU.add))
            chain(nc.vector.tensor_copy(decay_pow[:, 2 * P:3 * P], decay_pow[:, 0:P]))
            stats1(4, NT)

            def gates_out(i):
                dve.wait_ge(gab_done, i + 1)
                nc.vector.tensor_copy(gab[:, 2 * i:2 * i + 2, :].rearrange("p b d -> p (b d)"), bank[4 + i][:]).then_inc(gab_ready, 1)

            dve.wait_ge(gab_ready, 2)
            gates_out(2)
            gates_out(3)

            for b in range(1, B + 3):
                if b - 1 < B:
                    masked(b - 1)
                if b + 1 < B:
                    norm1(b + 1)
                if 0 <= b - 2 < B:
                    norm2(b - 2)
                if 0 <= b - 3:
                    top_logit(b - 3)
                if b - 1 < B:
                    attended(b - 1)
                    stats2(b - 1)
                    moments2(b - 1)
                if b == B + 1:
                    choose(0, NT - TPB)
            choose(NT - TPB, NT)

            dve.wait_ge(rank_done, 1)
            flat = lambda a: a[:].rearrange("p e t -> p (e t)")
            chain(nc.vector.tensor_tensor_scan(flat(upto), first0[:], bank[7][:, NT * E:2 * NT * E], 0.0,
                                               ALU.mult, ALU.add))
            chain(nc.vector.tensor_scalar(padded_cnt[:], upto[:, :, NT - 1], (P - 1) / 2, float(P << 23), ALU.add, ALU.add))
            chain(nc.vector.tensor_scalar(padded_cnt[:], padded_cnt[:], float(P << 23), None, ALU.subtract))
            nc.vector.tensor_tensor(flat(place), bank[7][:, 0:NT * E], flat(upto), ALU.add)
            chain(nc.vector.tensor_tensor_scan(ends[:], onef[:, 0:E], padded_cnt[:], 0.0, ALU.mult, ALU.add))
            chain(nc.vector.tensor_tensor(base[:], ends[:], padded_cnt[:], ALU.subtract))
            chain(nc.vector.tensor_tensor(place[:], place[:], base[:].unsqueeze(2).to_broadcast([P, E, NT]), ALU.add))
            chain(nc.vector.tensor_tensor(place[:], place[:], one_hot[:], ALU.mult))
            with nc.allow_low_precision(reason="whole numbers below 2^24"):
                nc.vector.tensor_reduce(pos[:], place[:].rearrange("p e t -> p t e"), AX_X, ALU.add).then_inc(pos_ready, 1)
            chain(nc.vector.tensor_tensor(past[:], ends[:, 0:E - 1].unsqueeze(1).to_broadcast([P, NR, E - 1]),
                                          tile_f[:], ALU.is_le))
            chain(nc.vector.tensor_reduce(expert[:, 4:NR + 4], past[:], AX_X, ALU.add))
            nc.vector.tensor_scalar(offsets[:, :, 0, :], expert[:, 3:3 + OG * RING].rearrange("p (g k) -> p g k", k=RING),
                                    float(2 * F), None, ALU.mult)
            nc.vector.tensor_scalar(offsets[:, :, 1, :], expert[:, 0:OG * RING].rearrange("p (g k) -> p g k", k=RING),
                                    float(FB * D), None, ALU.mult).then_inc(expert_ready, 1)

            def shared_act(h, f, s):
                dve.wait_ge(shsilu_ready, h + 1)
                nc.vector.tensor_tensor(acts[s][:, f * 512:(f + 1) * 512], bank[2 * f + 1][:], sg[f][:],
                                        ALU.mult).then_inc(shact_ready, 1)

            def shared_out(g, s):
                dve.wait_ge(shdown_done, g + 1)
                gb = gab[:, ds(g * BG, BG), D:2 * D]
                nc.vector.tensor_tensor(
                    shg[s][:].rearrange("p (b t d) -> p b t d", b=BG, t=TPB),
                    bank[4 + s][:].rearrange("p (b t d) -> p b t d", b=BG, t=TPB),
                    gb.unsqueeze(2).to_broadcast([P, BG, TPB, D]), ALU.mult).then_inc(shg_ready, 1)
                dve.wait_ge(shg_ready, g + 1)
                nc.vector.tensor_tensor(x1[:, ds(g * TG, TG), :], x1[:, ds(g * TG, TG), :],
                                        shg[s][:].rearrange("p (t d) -> p t d", t=TG), ALU.add).then_inc(base_ready, 1)

            with dve.Fori(0, G // 2) as i:
                for s in range(2):
                    for f in range(FB):
                        shared_act(i * 4 + (s * FB + f), f, s)
                for s in range(2):
                    shared_out(i * 2 + s, s)

            def act_out(j, s, early):
                dve.wait_ge(silu_e_ready, j + 1)
                if not early:
                    dve.wait_ge(actt_done, j - 1)
                nc.vector.tensor_tensor(acte[s][:], bank[s][:, F:2 * F], sge[s][:], ALU.mult).then_inc(act_ready, 1)

            def act_t_out(j, s, early):
                dve.wait_ge(actt_done, j + 1)
                if not early:
                    dve.wait_ge(down_done, j - 1)
                nc.vector.tensor_copy(act_t[s][:], bank[7][:, 0:F]).then_inc(act_t_ready, 1)

            def y_out(j, k, s, wave):
                dve.wait_ge(down_done, j + 1)
                if wave is not None:
                    dve.wait_ge(added[k], 16 * wave)
                nc.vector.tensor_tensor(y[k][:], bank[2 + s][:, 0:D], meta[:, ds(j, 1), 0:D].rearrange("p a d -> p (a d)"),
                                        ALU.mult).then_inc(y_ready, 1)

            act_out(0, 0, True)
            act_t_out(0, 0, True)
            act_out(1, 1, True)
            dve.wait_ge(meta_in, 32)
            for j in range(2, 2 + RING):
                act_t_out(j - 1, (j - 1) % 2, j - 1 < 2)
                act_out(j, j % 2, False)
                y_out(j - 2, (j - 2) % RING, j % 2, None)
            with dve.Fori(1, (NR - 3) // RING) as i:
                for k in range(RING):
                    j = i * RING + (2 + k)
                    act_t_out(j - 1, (k + 1) % 2, False)
                    act_out(j, k % 2, False)
                    y_out(j - 2, k, k % 2, i)
            j = NR - 1
            act_t_out(j - 1, (j - 1) % 2, False)
            act_out(j, j % 2, False)
            y_out(j - 2, (j - 2) % RING, j % 2, (j - 2) // RING)
            act_t_out(j, j % 2, False)
            y_out(j - 1, (j - 1) % RING, (j - 1) % 2, (j - 1) // RING)
            y_out(j, j % RING, j % 2, j // RING)

        @block.tensor
        def _(pe):
            pe.wait_ge(proj_in, 16)
            nc.tensor.matmul(bank[0][:, 0:D], projs[:, 0:D], projs[:, D:2 * D], start=True, stop=True)
            nc.tensor.matmul(bank[0][:, D:2 * D], projs[:, 2 * D:3 * D], projs[:, 3 * D:4 * D], start=True,
                             stop=True).then_inc(merge_done, 1)
            pe.wait_ge(mod_in, 16)
            pe.wait_ge(silu_ready, 1)
            for n, k in enumerate((0, 1, 3, 4)):
                last = nc.tensor.matmul(bank[1][:, n * B:(n + 1) * B], wmod[:, k * D:(k + 1) * D], siluc[:], start=True, stop=True)
            last.then_inc(mod_done, 1)
            nc.tensor.matmul(bank[2][0:B, 0:D], siluc[:], wmod[:, 2 * D:3 * D], start=True, stop=True)
            nc.tensor.matmul(bank[2][0:B, D:2 * D], siluc[:], wmod[:, 5 * D:6 * D], start=True, stop=True).then_inc(mod_done, 1)

            def t1(b):
                pe.wait_ge(xn1_ready, b + 1)
                if b >= 1:
                    pe.wait_ge(h_ready, b)
                for t in range(TPB):
                    last = nc.tensor.transpose(bank[0][:, t * P:(t + 1) * P], xn1[b % 2][:, t * D:(t + 1) * D], ident[:, 0:P])
                last.then_inc(t1_done, 1)

            def project(b):
                s = b % 2
                pe.wait_ge(h_ready, b + 1)
                pe.wait_ge(wvog_ready, b + 1)
                if b >= 1:
                    pe.wait_ge(vo_ready, b)
                    pe.wait_ge(q_ready, b)
                for t in range(TPB):
                    last = nc.tensor.matmul(bank[2][:, t * 256:t * 256 + D + 1], h_t[s][:, t * P:(t + 1) * P],
                                            wvog[:, b * (D + 2):b * (D + 2) + D + 1], start=True, stop=True)
                last.then_inc(vo_done, 1)
                nc.tensor.matmul(bank[1][:, 0:L], a_sb[:], h_t[s][:], start=True, stop=True).then_inc(q_done, 1)

            def scores(b):
                s = b % 2
                pe.wait_ge(q_ready, b + 1)
                if b >= 1:
                    pe.wait_ge(p_ready, b)
                nc.tensor.matmul(bank[3][:, 0:L], h_t[s][:, 0:P], q_t[s][:], start=True, stop=True)
                nc.tensor.matmul(bank[3][:, L:L + P], h_t[s][:, P:L], q_t[s][:, P:L], start=True, stop=True).then_inc(s_done, 1)

            def attend(b):
                s = b % 2
                pe.wait_ge(p_ready, b + 1)
                pe.wait_ge(vo_ready, b + 1)
                if b >= 1:
                    pe.wait_ge(x1_ready, b)
                else:
                    pe.wait_ge(gab_ready, B // 2)
                nc.tensor.matmul(bank[4][:, 0:D], p_t[s][:, 0:P], vo[s][:, 0:D], start=True, stop=True)
                nc.tensor.matmul(bank[4][:, D:2 * D], p_t[s][:, P:2 * P], vo[s][:, 0:D], start=True, stop=False)
                nc.tensor.matmul(bank[4][:, D:2 * D], p_t[s][:, 2 * P:3 * P], vo[s][:, D:2 * D], start=False,
                                 stop=True).then_inc(y_done, 1)

            def t2(b):
                pe.wait_ge(xn2_ready, b + 1)
                if b >= 1:
                    pe.wait_ge(h2_ready, b)
                for t in range(TPB):
                    last = nc.tensor.transpose(bank[5][:, t * P:(t + 1) * P], xn2[b % 2][:, t * D:(t + 1) * D], ident[:, 0:P])
                last.then_inc(t2_done, 1)

            def router(b):
                pe.wait_ge(h2_ready, b + 1)
                if b >= 1:
                    pe.wait_ge(top_ready, b)
                if b == B - 1:
                    pe.wait_ge(hot_ready, 1)
                for g in range(b * TPB, (b + 1) * TPB):
                    last = nc.tensor.matmul(bank[6][:, g * E:(g + 1) * E], h2_all[:, g * P:(g + 1) * P], gate_w,
                                            start=True, stop=True)
                last.then_inc(logit_done, 1)
                if b >= 1:
                    pe.wait_ge(xs_ready, b)
                for t in range(TPB):
                    g = b * TPB + t
                    last = nc.tensor.transpose(bank[7][:, t * D:(t + 1) * D], h2_all[:, g * P:(g + 1) * P], ident[:, 0:P])
                last.then_inc(t3_done, 1)

            def shared_first(f):
                pe.wait_ge(shared_in, 32)
                for u in range(2):
                    last = nc.tensor.matmul(bank[2 * f + u][:], wgu[:, SH + u * F + f * P:SH + u * F + (f + 1) * P],
                                            h2_all[:, 0:512], start=True, stop=True)
                last.then_inc(shgu_done, 1)

            def spread(i):
                for b in (2 * i, 2 * i + 1):
                    last = nc.tensor.matmul(bank[4 + i][:, (b % 2) * 256:(b % 2) * 256 + 256],
                                            ident[0:B, b:b + 1].to_broadcast([B, P]), grow[:], start=True, stop=True)
                last.then_inc(gab_done, 1)

            pe.wait_ge(const_ready, 1)
            pe.wait_ge(merge_ready, 1)
            t1(0)
            pe.wait_ge(grow_ready, 1)
            spread(0)
            pe.wait_ge(wg_ready, 1)
            for b in range(B + 3):
                if b < B and b > 0:
                    t1(b)
                if 0 <= b - 1 < B:
                    scores(b - 1)
                if b >= 3:
                    t2(b - 3)
                if b < B:
                    project(b)
                if b == 0:
                    for i in range(1, B // 2):
                        spread(i)
                if b >= 3:
                    router(b - 3)
                if 0 <= b - 1 < B:
                    attend(b - 1)
                if b == B:
                    shared_first(0)
                if b == B + 1:
                    shared_first(1)

            pe.wait_ge(shared_in, 32)

            def shared_up(i, s):
                g = i * 2 + s
                for f in range(FB):
                    if s:
                        pe.wait_ge(shact_ready, i * 4 + (s * FB + f - 1))
                    for u in range(2):
                        last = nc.tensor.matmul(bank[2 * f + u][:],
                                                wgu[:, SH + u * F + f * P:SH + u * F + (f + 1) * P],
                                                h2_all[:, ds(g * 512, 512)], start=True, stop=True)
                    last.then_inc(shgu_done, 1)

            def shared_down(i, s):
                pe.wait_ge(shact_ready, i * 4 + (s * FB + FB))
                for t in range(TG):
                    for f in range(FB):
                        last = nc.tensor.matmul(bank[4 + s][:, t * D:(t + 1) * D],
                                                acts[s][:, f * 512 + t * P:f * 512 + (t + 1) * P],
                                                wdn[:, SHD + f * D:SHD + (f + 1) * D], start=(f == 0), stop=(f == FB - 1))
                last.then_inc(shdown_done, 1)

            pe.wait_ge(hot_ready, 2)
            hot = one_hot[:].rearrange("p e t -> p (e t)")
            pe.wait_ge(xs_ready, B)
            nc.tensor.matmul(bank[7][:, 0:NT * E], upto_self[:], hot, start=True, stop=True)
            nc.tensor.matmul(bank[7][:, NT * E:2 * NT * E], oneb[:], hot, start=True, stop=True).then_inc(rank_done, 1)
            shared_up(0, 1)
            for s in range(2):
                shared_down(0, s)
            with pe.Fori(1, G // 2) as i:
                for s in range(2):
                    shared_up(i, s)
                for s in range(2):
                    shared_down(i, s)

            pe.wait_ge(expert_ready, 1)
            pe.wait_ge(routed_in, 32)

            def t_rows(j, k, wave, early):
                pe.wait_ge(rows_in[k], 16 * wave)
                if not early:
                    pe.wait_ge(xs_t_ready, j)
                nc.tensor.transpose(bank[6][:, 0:P], rows[k][:], ident[:, 0:P]).then_inc(xr_done, 1)

            def gate_up(j, s, early, offset):
                pe.wait_ge(xs_t_ready, j + 1)
                if not early:
                    pe.wait_ge(act_ready, j - 1)
                nc.tensor.matmul(bank[s][:], xs_t[s][:], wgu[:, ds(offset, 2 * F)], start=True, stop=True).then_inc(gu_done, 1)

            def t_act(j, s, early):
                pe.wait_ge(act_ready, j + 1)
                if not early:
                    pe.wait_ge(act_t_ready, j)
                for f in range(FB):
                    last = nc.tensor.transpose(bank[7][:, f * P:(f + 1) * P], acte[s][:, f * P:(f + 1) * P], ident[:, 0:P])
                last.then_inc(actt_done, 1)

            def down(j, s, early, offset):
                pe.wait_ge(act_t_ready, j + 1)
                if not early:
                    pe.wait_ge(y_ready, j - 1)
                for f in range(FB):
                    last = nc.tensor.matmul(bank[2 + s][:, 0:D], act_t[s][:, f * P:(f + 1) * P],
                                            wdn[:, ds(offset + f * D, D)], start=(f == 0), stop=(f == FB - 1))
                last.then_inc(down_done, 1)

            def load_offsets(g):
                _, values = nc.values_load_multi_w_load_instructions(
                    offsets[0:1, ds(g, 1), :, :].rearrange("p a u k -> p (a u k)"), engines=(mybir.EngineType.PE,),
                    min_val=0, max_val=(E - 1) * 2 * F,
                    skip_runtime_bounds_check_because="an expert number is a count of at most E - 1 ends")
                return ([v.with_bounds(min_val=0, max_val=(E - 1) * 2 * F) for v in values[0:RING]],
                        [v.with_bounds(min_val=0, max_val=(E - 1) * FB * D) for v in values[RING:2 * RING]])

            def tile_step(j, s, k, wave, up, dn, early=False):
                t_act(j - 2, s, False)
                down(j - 3, 1 - s, early, dn)
                t_rows(j + 1, k, wave, False)
                gate_up(j, s, False, up)

            up_offset, down_offset = load_offsets(0)
            t_rows(0, 0, 1, True)
            for j in range(3):
                if j == 2:
                    t_act(0, 0, True)
                t_rows(j + 1, j + 1, 1, False)
                gate_up(j, j % 2, j < 2, up_offset[j + 1])
            up_offset, down_offset = load_offsets(1)
            for j in range(3, 3 + RING):
                tile_step(j, j % 2, (j + 1) % RING, 1 + (j + 1) // RING, up_offset[j - 3], down_offset[j - 3], j < 5)
            with pe.Fori(1, (NR - 4) // RING) as i:
                up_offset, down_offset = load_offsets(i + 1)
                for k in range(RING):
                    tile_step(i * RING + (3 + k), (k + 1) % 2, k, i + 2, up_offset[k], down_offset[k])
            for j in range(3 + (NR - 4) // RING * RING, NR + 3):
                if (j + 1) % RING == 0:
                    up_offset, down_offset = load_offsets((j + 1) // RING)
                if j - 2 < NR:
                    t_act(j - 2, j % 2, False)
                down(j - 3, (j + 1) % 2, False, down_offset[(j + 1) % RING])
                if j + 1 < NR:
                    t_rows(j + 1, (j + 1) % RING, 1 + (j + 1) // RING, False)
                if j < NR:
                    gate_up(j, j % 2, False, up_offset[(j + 1) % RING])


def kernel(**inputs):
    import numpy as np
    import concourse.bacc as bacc
    from concourse import mybir as mb
    from concourse.bass_utils import run_bass_kernel_spmd

    a = {k: np.asarray(v) for k, v in inputs.items()}
    at, ff = "L0_attn_", "L0_ffn_"
    gates = np.concatenate([a[ff + "r_gate"], a[ff + "shared_gate"][None]])
    ups = np.concatenate([a[ff + "r_up"], a[ff + "shared_up"][None]])
    downs = np.concatenate([a[ff + "r_down"], a[ff + "shared_down"][None]])
    arrays = {
        "x": a[at + "x"],
        "proj": np.concatenate([a[at + "Wq"].T, a[at + "Wk"].T, a[at + "Wv"].T, a[at + "Wo"]], axis=1),
        "row": np.concatenate([a[at + "bo"], a[at + "bg"], a[at + "decay_param"]]),
        "modin": np.concatenate([a["L0_c"].T, a["L0_wmod"], a[at + "Wg"], a[ff + "gate_w"].T], axis=1),
        "w_gu": np.concatenate([gates, ups], axis=1).transpose(2, 0, 1).reshape(D, -1),
        "w_down": downs.transpose(0, 2, 1).reshape(E + 1, FB, P, D).transpose(2, 0, 1, 3).reshape(P, -1),
    }
    arrays = {k: np.ascontiguousarray(v) for k, v in arrays.items()}
    nc = bacc.Bacc("TRN2", target_bir_lowering=False, num_devices=1)
    args = [nc.dram_tensor(k, v.shape, mb.dt.from_np(v.dtype), kind="ExternalInput").ap() for k, v in arrays.items()]
    out = nc.dram_tensor("out", (B, L, D), F32, kind="ExternalOutput").ap()
    adaln_block(nc, *args, out)
    return run_bass_kernel_spmd(nc, [arrays], core_ids=[0]).results[0]["out"]
```

```python
from contextlib import ExitStack

import concourse.bass as bass
from concourse import mybir

F32 = mybir.dt.float32
BF16 = mybir.dt.bfloat16
I32 = mybir.dt.int32
ACT = mybir.ActivationFunctionType
ALU = mybir.AluOpType
AX_X = mybir.AxisListType.X

P = 128
B, L, D = 8, 256, 128
M = 64
F, E = 256, 8
FB = F // P
TPB = L // P
NT = B * TPB
NV = NT + E - 1
ROW = 2 * D + 1
G, TG = 4, NT // 4
BG = B // G
RING = 4
OG = -(-(NV + 4) // RING)
CHUNKS = [(0, 1), (1, 2), (2, 4), (4, 8), (8, 12), (12, 16)]
GATE_BANK, UP_BANK = (0, 2, 5), (1, 3, 4)
CHUNK_BANK = (4, 5, 6, 4, 5, 6)
EPS = 1e-5
DECAY_MIN, DECAY_MAX = 0.9, 0.999
ds = bass.ds


def adaln_block(nc, x, proj, row, c, modin, w_gu, w_down, out):
    sorted_rows = nc.dram_tensor("sorted_rows", (NT * P, ROW), F32).ap()
    gate_rows = nc.dram_tensor("gate_rows", (2, B, D), F32).ap()

    with ExitStack() as ctx:
        def sb(name, shape, dt=F32):
            return ctx.enter_context(nc.sbuf_tensor(name, shape, dt))

        def sem(name):
            return ctx.enter_context(nc.semaphore(name))

        bank = [ctx.enter_context(nc.psum_tensor(f"bank{i}", [P, 512], F32)) for i in range(8)]

        x_all = sb("x_all", [P, NT, D])
        projs = sb("projs", [M, 4 * D])
        rowb = sb("rowb", [P, D + 2])
        c_in = sb("c_in", [P, B])
        mods = sb("mods", [P, 6 * D + 1 + E])
        wgu = sb("wgu", [P, (E + 1) * 2 * F])
        wdn = sb("wdn", [P, (E + 1) * FB * D])
        c_t = c_in[:]
        wmod = mods[:, 0:6 * D]
        wg_col = mods[:, 6 * D:1 + 6 * D]
        gate_w = mods[:, 1 + 6 * D:1 + 6 * D + E]

        onef = sb("onef", [P, 2 * P])
        ident = sb("ident", [P, 2 * P])
        upto_self = sb("upto_self", [P, P], BF16)
        oneb = sb("oneb", [P, P], BF16)
        rev_i = sb("rev_i", [P, E], I32)
        rev = sb("rev", [P, E])
        tile_end_i = sb("tile_end_i", [P, NT - 1], I32)
        tile_end = sb("tile_end", [P, NT - 1])
        before_i = sb("before_i", [P, NV], I32)
        before = sb("before", [P, NV])
        tiles_i = sb("tiles_i", [P, NT - 1], I32)
        tiles_f = sb("tiles_f", [P, NT - 1])
        row_i = sb("row_i", [P, E - 1], I32)
        row_f = sb("row_f", [P, E - 1])
        first0 = sb("first0", [P, E * NT])
        mhalf = sb("mhalf", [P, NT])
        eps = sb("eps", [P, TPB])

        sigs = sb("sigs", [P, 9])
        warm = sb("warm", [P, 1])
        siluc = sb("siluc", [P, 8])
        decay = sb("decay", [P, 1])
        decay_pow = sb("decay_pow", [P, 3 * P])
        shsc = sb("shsc", [P, 4, B])
        gneg = sb("gneg", [B, D])
        gabs = sb("gabs", [B, D])
        gsign = sb("gsign", [B, D])
        grow = sb("grow", [B, 2 * D])
        ga_all = sb("ga_all", [P, B, D])
        gb_all = sb("gb_all", [P, B, D])
        ga_first = sb("ga_first", [P, 2, D])
        gabo = sb("gabo", [P, B, D])
        a_sb = sb("a_sb", [P, D])
        wvo = sb("wvo", [P, D])
        wvog = sb("wvog", [P, B * (D + 2)])
        st1 = sb("st1", [P, NT, 6])
        mv1 = sb("mv1", [P, NT, 2])
        ve1 = sb("ve1", [P, NT])
        rstd1 = sb("rstd1", [P, NT])

        xn1 = [sb(f"xn1_{s}", [P, L]) for s in range(2)]
        h_t = [sb(f"h_t{s}", [P, L]) for s in range(2)]
        q_t = [sb(f"q_t{s}", [P, L]) for s in range(2)]
        gate = [sb(f"gate{s}", [P, TPB]) for s in range(2)]
        gate2 = [sb(f"gate2_{s}", [P, TPB]) for s in range(2)]
        vo = [sb(f"vo{s}", [P, L]) for s in range(2)]
        p_t = [sb(f"p_t{s}", [P, 3 * P]) for s in range(2)]
        st2 = [sb(f"st2_{s}", [P, TPB, 6]) for s in range(2)]
        mv2 = [sb(f"mv2_{s}", [P, TPB, 2]) for s in range(2)]
        ve2 = [sb(f"ve2_{s}", [P, TPB]) for s in range(2)]
        rstd2 = [sb(f"rstd2_{s}", [P, TPB]) for s in range(2)]
        xn2 = [sb(f"xn2_{s}", [P, L]) for s in range(2)]
        score = [sb(f"score{s}", [P, TPB]) for s in range(2)]
        xb = sb("xb", [P, B * L])
        x1 = sb("x1", [P, NT, D])
        h2_all = sb("h2_all", [P, B * L])
        pay = sb("pay", [P, NT, ROW])

        top = sb("top", [P, NT])
        eq = sb("eq", [P, NT, E])
        cand = sb("cand", [P, NT, E])
        best = sb("best", [P, NT])
        one_hot = sb("one_hot", [P, E, NT], BF16)
        upto = sb("upto", [P, E, NT])
        ends = sb("ends", [P, E])
        base = sb("base", [P, E])
        place = sb("place", [P, E, NT])
        pos = sb("pos", [P, NT], I32)
        ended = sb("ended", [P, NT - 1, E - 1])
        boundary = sb("boundary", [P, NT - 1])
        passed = sb("passed", [P, NV, NT - 1])
        tile = sb("tile", [P, NV])
        tile_start = sb("tile_start", [P, OG * RING])
        expert = sb("expert", [P, OG * RING])
        ends_row = sb("ends_row", [P, E - 1])
        behind = sb("behind", [P, NV, E - 1])
        owner = sb("owner", [P, NV])
        mask = sb("mask", [P, NV])
        offsets = sb("offsets", [P, OG, 2, RING], I32)
        weights_at = sb("weights_at", [P, NV + 1], I32)
        sum_at = sb("sum_at", [P, NV + 1], I32)

        sg = [sb(f"sg{f}", [P, 512]) for f in range(FB)]
        acts = [sb(f"acts{s}", [P, FB * 512]) for s in range(2)]
        shg = [sb(f"shg{s}", [P, 512]) for s in range(2)]

        rows = sb("rows", [P, NT, ROW])
        xs_all = sb("xs_all", [P, NT * P])
        routed = sb("routed", [P, NT * D])
        w_now = [sb(f"w_now{k}", [P, 2 * F]) for k in range(RING)]
        sge = [sb(f"sge{s}", [P, F]) for s in range(2)]
        acte = [sb(f"acte{s}", [P, F]) for s in range(2)]
        y = [sb(f"y{k}", [P, D]) for k in range(RING)]

        c_landed, row_in, proj_in = sem("c_landed"), sem("row_in"), sem("proj_in")
        mod_gate_in, mod_in = sem("mod_gate_in"), sem("mod_in")
        x_in = [sem(f"x_in{i}") for i in range(4)]
        shared_in, routed_in = sem("shared_in"), sem("routed_in")
        scattered = sem("scattered")
        base_out = sem("base_out")
        rows_in = [sem(f"rows_in{n}") for n in range(len(CHUNKS))]
        added = [sem(f"added{k}") for k in range(RING)]
        const_step, const_ready = sem("const_step"), sem("const_ready")
        sig_ready, setup_step = sem("sig_ready"), sem("setup_step")
        silu_ready, mod_done, mod_ready = sem("silu_ready"), sem("mod_done"), sem("mod_ready")
        merge_done, merge_ready = sem("merge_done"), sem("merge_ready")
        grow_ready, ga_done, ga_ready = sem("grow_ready"), sem("ga_done"), sem("ga_ready")
        grow_out = [sem("ga_out"), sem("gb_out")]
        gab_in = [sem("ga_in"), sem("gb_all_in")]
        wg_ready, wvog_ready, gabo_ready = sem("wg_ready"), sem("wvog_ready"), sem("gabo_ready")
        decay_ready = sem("decay_ready")
        stat1_ready, ve1_ready, rstd1_ready = sem("stat1_ready"), sem("ve1_ready"), sem("rstd1_ready")
        xn1_ready, t1_done, h_ready = sem("xn1_ready"), sem("t1_done"), sem("h_ready")
        q_done, q_ready, vo_done, vo_ready = sem("q_done"), sem("q_ready"), sem("vo_done"), sem("vo_ready")
        gate_step, gate2_step = sem("gate_step"), sem("gate2_step")
        s_done, p_ready, y_done = sem("s_done"), sem("p_ready"), sem("y_done")
        xb_ready, x1_ready, st2_step = sem("xb_ready"), sem("x1_ready"), sem("st2_step")
        mv2_ready, ve2_step, rstd2_ready = sem("mv2_ready"), sem("ve2_step"), sem("rstd2_ready")
        xn2_ready, t2_done, h2_ready = sem("xn2_ready"), sem("t2_done"), sem("h2_ready")
        logit_done, top_ready, score_ready = sem("logit_done"), sem("top_ready"), sem("score_ready")
        t3_done, xs_ready, gb_in = sem("t3_done"), sem("xs_ready"), sem("gb_in")
        route_step, hot_ready, rank_done = sem("route_step"), sem("hot_ready"), sem("rank_done")
        pos_ready, visits_ready = sem("pos_ready"), sem("visits_ready")
        shgu_done, shsilu_ready, shact_ready = sem("shgu_done"), sem("shsilu_ready"), sem("shact_ready")
        shdown_done, shg_ready, base_ready = sem("shdown_done"), sem("shg_ready"), sem("base_ready")
        xr_done, xr_ready = sem("xr_done"), sem("xr_ready")
        w_ready, gu_done, silu_e_ready = sem("w_ready"), sem("gu_done"), sem("silu_e_ready")
        act_ready, down_done, sum_ready = sem("act_ready"), sem("down_done"), sem("sum_ready")
        y_ready = sem("y_ready")

        block = ctx.enter_context(nc.Block())

        x_tiles = x.rearrange("b (t p) d -> p (b t) d", p=P)
        out_tiles = out.rearrange("b (t p) d -> p (b t) d", p=P)
        out_rows = out.rearrange("b l d -> (b l) d")
        sorted_tiles = sorted_rows.rearrange("(j p) c -> p j c", p=P)
        SH = E * 2 * F
        SHD = E * FB * D

        @block.sync
        def _(sp):
            sp.dma_start(c_in[:], c).then_inc(c_landed, 16)
            sp.dma_start(mods[:, 0:2 * D], modin[:, 0:2 * D]).then_inc(mod_gate_in, 16)
            sp.dma_start(x_all[:, 0:4, :], x_tiles[:, 0:4, :]).then_inc(x_in[0], 16)
            sp.dma_start(mods[:, 2 * D:], modin[:, 2 * D:]).then_inc(mod_in, 16)
            for i in range(1, 4):
                sp.dma_start(x_all[:, 4 * i:4 * i + 4, :], x_tiles[:, 4 * i:4 * i + 4, :]).then_inc(x_in[i], 16)
            sp.dma_start(wgu[:, SH:], w_gu[:, SH:]).then_inc(shared_in, 16)
            sp.dma_start(wdn[:, SHD:], w_down[:, SHD:]).then_inc(shared_in, 16)
            for h in range(2):
                sp.wait_ge(grow_ready, h + 1)
                sp.dma_start(gate_rows[h], grow[:, h * D:(h + 1) * D]).then_inc(grow_out[h], 16)
            for h, full in ((0, ga_all), (1, gb_all)):
                sp.wait_ge(grow_out[h], 16)
                sp.dma_start(full[:].rearrange("p b d -> p (b d)"),
                             gate_rows[h].rearrange("b d -> (b d)").partition_broadcast(P)).then_inc(gab_in[h], 16)
            sp.dma_start(wgu[:, 0:SH], w_gu[:, 0:SH]).then_inc(routed_in, 16)
            sp.dma_start(wdn[:, 0:SHD], w_down[:, 0:SHD]).then_inc(routed_in, 16)
            sp.wait_ge(gab_in[1], 16)
            for t in range(TPB):
                sp.dma_start(pay[:, t:NT:TPB, D:2 * D], gb_all[:]).then_inc(gb_in, 16)
            def base(g):
                sp.wait_ge(base_ready, g + 1)
                sp.dma_start(out_tiles[:, g * TG:(g + 1) * TG, :], x1[:, g * TG:(g + 1) * TG, :]).then_inc(base_out, 16)

            base(0)
            base(1)
            sp.wait_ge(scattered, 16 * NT)
            for n, (lo, hi) in enumerate(CHUNKS):
                sp.dma_start(rows[:, lo:hi, :], sorted_tiles[:, lo:hi, :]).then_inc(rows_in[n], 16)
            base(2)
            base(3)
            sp.wait_ge(base_out, 16 * G)
            for k in range(RING):
                sp.wait_ge(added[k], 16 * (NT // RING))

        @block.gpsimd
        def _(pool):
            nc.gpsimd.memset(onef[:], 1.0).then_inc(const_step, 1)
            pool.wait_ge(const_step, 1)
            nc.gpsimd.affine_select(out=ident[:], in_=onef[:], compare_op=ALU.is_equal, fill=0.0, base=0,
                                    pattern=[[-1, 2 * P]], channel_multiplier=1)
            nc.gpsimd.memset(mhalf[:], -0.5)
            nc.gpsimd.memset(eps[:], EPS).then_inc(const_ready, 1)
            nc.gpsimd.memset(oneb[:], 1.0).then_inc(const_step, 1)
            nc.gpsimd.memset(upto_self[:], -1.0).then_inc(const_step, 1)
            pool.wait_ge(const_step, 3)
            nc.gpsimd.affine_select(out=upto_self[:], in_=upto_self[:], compare_op=ALU.is_ge, fill=0.0, base=0,
                                    pattern=[[-1, P]], channel_multiplier=1)
            nc.gpsimd.iota(rev_i[:], pattern=[[-1, E]], base=E, channel_multiplier=0)
            nc.gpsimd.iota(tile_end_i[:], pattern=[[P, NT - 1]], base=P, channel_multiplier=0)
            nc.gpsimd.iota(before_i[:], pattern=[[1, NV]], base=-1, channel_multiplier=0)
            nc.gpsimd.iota(tiles_i[:], pattern=[[1, NT - 1]], base=0, channel_multiplier=0)
            nc.gpsimd.iota(row_i[:], pattern=[[0, E - 1]], base=0, channel_multiplier=1)
            nc.gpsimd.iota(pay[:, :, 2 * D:ROW].bitcast(I32), pattern=[[P, NT]], base=0,
                           channel_multiplier=1)
            nc.gpsimd.memset(first0[:], 1.0).then_inc(const_step, 1)
            pool.wait_ge(const_step, 4)
            nc.gpsimd.tensor_copy(rev[:], rev_i[:])
            nc.gpsimd.tensor_copy(tile_end[:], tile_end_i[:])
            nc.gpsimd.tensor_copy(before[:], before_i[:])
            nc.gpsimd.tensor_copy(tiles_f[:], tiles_i[:])
            nc.gpsimd.tensor_copy(row_f[:], row_i[:])
            nc.gpsimd.memset(first0[:, 0:E * NT:NT], 0.0)
            nc.gpsimd.memset(weights_at[:], 0)
            nc.gpsimd.memset(tile_start[:], 0.0)
            nc.gpsimd.memset(sum_at[:], 0)
            nc.gpsimd.memset(expert[:], 0.0).then_inc(const_ready, 1)

            def rstd_first(part, lo, hi):
                pool.wait_ge(stat1_ready, part + 1)
                nc.gpsimd.tensor_scalar(ve1[:, lo:hi], mv1[:, lo:hi, 1], EPS, None, ALU.add).then_inc(ve1_ready, 1)
                pool.wait_ge(ve1_ready, part + 1)
                nc.gpsimd.tensor_tensor(rstd1[:, lo:hi], ve1[:, lo:hi], mhalf[:, lo:hi], ALU.pow).then_inc(rstd1_ready, 1)

            wv = wvog[:].rearrange("p (b n) -> p b n", b=B)

            def weights(b):
                if b < 2:
                    pool.wait_ge(ga_ready, 1)
                    ga = ga_first[:, b, :]
                else:
                    pool.wait_ge(gab_in[0], 16)
                    ga = ga_all[:, b, :]
                nc.gpsimd.tensor_tensor(wv[:, b, 0:D], ga, wvo[:], ALU.mult).then_inc(wvog_ready, 1)

            def residual(b):
                ga = ga_first[:, b, :] if b < 2 else ga_all[:, b, :]
                nc.gpsimd.tensor_tensor(gabo[:, b, :], ga, rowb[:, 0:D], ALU.mult).then_inc(gabo_ready, 1)
                pool.wait_ge(gabo_ready, b + 1)
                nc.gpsimd.tensor_tensor(
                    xb[:, b * L:(b + 1) * L].rearrange("p (t d) -> p t d", t=TPB), x_all[:, b * TPB:(b + 1) * TPB, :],
                    gabo[:, b:b + 1, :].to_broadcast([P, TPB, D]), ALU.add).then_inc(xb_ready, 1)

            def rstd(b):
                s = b % 2
                pool.wait_ge(mv2_ready, b + 1)
                nc.gpsimd.tensor_tensor(ve2[s][:], mv2[s][:, :, 1], eps[:, 0:TPB], ALU.add).then_inc(ve2_step, 1)
                pool.wait_ge(ve2_step, b + 1)
                nc.gpsimd.tensor_tensor(rstd2[s][:], ve2[s][:], mhalf[:, 0:TPB], ALU.pow).then_inc(rstd2_ready, 1)

            rstd_first(0, 0, 4)
            pool.wait_ge(mod_in, 16)
            nc.gpsimd.tensor_copy(wv[:, :, D], wg_col.to_broadcast([P, B])).then_inc(wg_ready, 1)
            pool.wait_ge(merge_ready, 1)
            weights(0)
            weights(1)
            pool.wait_ge(row_in, 16)
            for i in range(4):
                pool.wait_ge(x_in[i], 16)
            residual(0)
            rstd_first(1, 4, 8)
            weights(2)
            residual(1)
            rstd_first(2, 8, NT)
            rstd(0)
            for b in range(1, B):
                if b + 2 < B:
                    weights(b + 2)
                if b + 1 < B:
                    residual(b + 1)
                if b == B - 2:
                    nc.gpsimd.memset(routed[:], 0.0).then_inc(const_ready, 1)
                rstd(b)
            pool.wait_ge(pos_ready, 1)
            pool.wait_ge(gb_in, 16 * TPB)
            for t in range(NT):
                if t == 0:
                    pool.wait_ge(xs_ready, B - 1)
                if t == NT - TPB:
                    pool.wait_ge(xs_ready, B)
                nc.gpsimd.indirect_dma_start(sorted_rows, bass.IndirectOffsetOnAxis(pos[:, t:t + 1], 0),
                                             pay[:, t, :], None).then_inc(scattered, 16)
            pool.wait_ge(base_out, 16 * G)
            for t in range(NT):
                pool.wait_ge(y_ready, t + 1)
                nc.gpsimd.indirect_dma_start(out_rows, bass.IndirectOffsetOnAxis(rows[:, t, 2 * D:ROW].bitcast(I32), 0),
                                             y[t % RING][:], None, compute_op=ALU.add).then_inc(added[t % RING], 16)

        @block.scalar
        def _(act):
            act.wait_ge(const_step, 1)
            nc.scalar.activation(warm[:], onef[:, 0:1], ACT.Sigmoid)
            act.dma_start(rowb[:], row.partition_broadcast(P)).then_inc(row_in, 16)
            act.dma_start(projs[:], proj).then_inc(proj_in, 16)
            act.wait_ge(c_landed, 16)
            nc.scalar.activation(sigs[:, 0:8], c_t, ACT.Sigmoid).then_inc(sig_ready, 1)
            act.wait_ge(row_in, 16)
            nc.scalar.activation(sigs[:, 8:9], rowb[:, D + 1:D + 2], ACT.Sigmoid).then_inc(sig_ready, 1)
            act.wait_ge(merge_done, 1)
            nc.scalar.copy(a_sb[:], bank[3][:, 0:D])
            nc.scalar.copy(wvo[:], bank[3][:, D:2 * D]).then_inc(merge_ready, 1)

            def h_out(b):
                act.wait_ge(t1_done, b + 1)
                if b >= 2:
                    act.wait_ge(s_done, b - 1)
                    act.wait_ge(vo_done, b - 1)
                nc.scalar.activation(h_t[b % 2][:], bank[0][:, 0:L], ACT.Identity, bias=shsc[:, 0, b:b + 1],
                                     scale=shsc[:, 1, b:b + 1]).then_inc(h_ready, 1)

            def h2_out(b):
                if b == 0:
                    act.wait_ge(mod_ready, 2)
                act.wait_ge(t2_done, b + 1)
                nc.scalar.activation(h2_all[:, b * L:(b + 1) * L], bank[5][:, 0:L], ACT.Identity,
                                     bias=shsc[:, 2, b:b + 1], scale=shsc[:, 3, b:b + 1]).then_inc(h2_ready, 1)

            def gate_out(b):
                act.wait_ge(vo_done, b + 1)
                nc.scalar.activation(gate[b % 2][:], bank[2][:].rearrange("p (t n) -> p t n", t=TPB)[:, :, D],
                                     ACT.Sigmoid, bias=rowb[:, D:D + 1]).then_inc(gate_step, 1)

            def q_out(b):
                act.wait_ge(q_done, b + 1)
                nc.scalar.copy(q_t[b % 2][:], bank[1][:, 0:L]).then_inc(q_ready, 1)

            def gate2_out(b):
                act.wait_ge(gate_step, b + 1)
                nc.scalar.activation(gate2[b % 2][:], gate[b % 2][:], ACT.Square).then_inc(gate2_step, 1)

            def score_out(b):
                act.wait_ge(top_ready, b + 1)
                nc.scalar.activation(score[b % 2][:], top[:, b * TPB:(b + 1) * TPB], ACT.Sigmoid).then_inc(score_ready, 1)

            def vo_out(b):
                s = b % 2
                act.wait_ge(gate2_step, b + 1)
                if b >= 2:
                    act.wait_ge(y_done, b - 1)
                for t in range(TPB):
                    last = nc.scalar.mul(vo[s][:, t * D:(t + 1) * D], bank[2][:, t * 256:t * 256 + D],
                                         gate2[s][:, t:t + 1])
                last.then_inc(vo_ready, 1)

            def xs_out(b):
                act.wait_ge(score_ready, b + 1)
                act.wait_ge(t3_done, b + 1)
                for t in range(TPB):
                    last = nc.scalar.mul(pay[:, b * TPB + t, 0:D], bank[7][:, t * D:(t + 1) * D],
                                         score[b % 2][:, t:t + 1])
                last.then_inc(xs_ready, 1)

            act.wait_ge(mod_ready, 1)
            for b in range(B + 3):
                if b == 0:
                    act.wait_ge(ga_done, 1)
                    nc.scalar.copy(ga_first[:].rearrange("p b d -> p (b d)"), bank[4][:, 0:2 * D]).then_inc(ga_ready, 1)
                if b < B:
                    h_out(b)
                if b >= 3:
                    h2_out(b - 3)
                if b < B:
                    gate_out(b)
                    q_out(b)
                    gate2_out(b)
                if b >= 3:
                    score_out(b - 3)
                if b < B:
                    vo_out(b)
                if b >= 3:
                    xs_out(b - 3)

            def shared_silu(h):
                act.wait_ge(shgu_done, h + 1)
                if h >= FB:
                    act.wait_ge(shact_ready, h - 1)
                nc.scalar.activation(sg[h % FB][:], bank[GATE_BANK[h % 3]][:], ACT.Silu).then_inc(shsilu_ready, 1)

            for h in range(G * FB):
                shared_silu(h)

            def rows_t_out(n):
                lo, hi = CHUNKS[n]
                act.wait_ge(xr_done, n + 1)
                nc.scalar.copy(xs_all[:, lo * P:hi * P], bank[CHUNK_BANK[n]][:, 0:(hi - lo) * P]).then_inc(xr_ready, 1)

            def load_weights_at(g):
                _, values = nc.values_load_multi_w_load_instructions(
                    weights_at[0:1, ds(g * RING, RING)], engines=(mybir.EngineType.Activation,),
                    min_val=0, max_val=(E - 1) * 2 * F, skip_runtime_bounds_check_because="an expert's weights' start")
                return values

            def weights_out(v, s, start):
                if not isinstance(v, int) or v >= RING:
                    act.wait_ge(gu_done, v - RING + 1)
                nc.scalar.copy(w_now[s][:], wgu[:, ds(start, 2 * F)]).then_inc(w_ready, 1)

            def silu_out(v, s):
                act.wait_ge(gu_done, v + 1)
                if not isinstance(v, int) or v >= 2:
                    act.wait_ge(act_ready, v - 1)
                nc.scalar.activation(sge[s][:], bank[s][:, 0:F], ACT.Silu).then_inc(silu_e_ready, 1)

            act.wait_ge(routed_in, 32)
            act.wait_ge(visits_ready, 1)
            starts = load_weights_at(0)
            for v in range(RING):
                weights_out(v, v, starts[v])
            rows_t_out(0)
            rows_t_out(1)
            for v in range(2 + RING):
                if v == 1:
                    rows_t_out(2)
                if v >= 2:
                    if v == 2:
                        starts = load_weights_at(1)
                    weights_out(v + 2, (v + 2) % RING, starts[v - 2])
                silu_out(v, v % 2)
                if v in (2, 3, 4):
                    rows_t_out(v + 1)
            with act.Fori(1, (NV - 4) // RING) as i:
                starts = load_weights_at(i + 1)
                for k in range(RING):
                    v = i * RING + (2 + k)
                    weights_out(v + 2, k, starts[k])
                    silu_out(v, k % 2)
            for v in range(2 + (NV - 4) // RING * RING, NV):
                if (v + 2) % RING == 0 and v + 2 < NV:
                    starts = load_weights_at((v + 2) // RING)
                if v + 2 < NV:
                    weights_out(v + 2, (v + 2) % RING, starts[(v + 2) % RING])
                silu_out(v, v % 2)

        @block.vector
        def _(dve):
            steps = [0]

            def chain(ins, signal=setup_step):
                steps[0] += 1
                ins.then_inc(signal, 1)
                dve.wait_ge(signal, steps[0])

            def stats1(lo, hi):
                for t in range(lo, hi):
                    if t % 4 == 0:
                        dve.wait_ge(x_in[t // 4], 16)
                    last = nc.vector.bn_stats(st1[:, t, :], x_all[:, t, :])
                chain(last)
                for t in range(lo, hi):
                    last = nc.vector.bn_aggr(mv1[:, t, :], st1[:, t, :])
                last.then_inc(stat1_ready, 1)

            logits = bank[6][:, 0:NT * E].rearrange("p (t e) -> p t e", t=NT)

            def choose(lo, hi):
                n = hi - lo
                if lo == 0:
                    dve.wait_ge(const_ready, 2)
                dve.wait_ge(top_ready, hi // TPB)
                chain(nc.vector.tensor_tensor(eq[:, lo:hi, :], logits[:, lo:hi, :],
                                              top[:, lo:hi].unsqueeze(2).to_broadcast([P, n, E]), ALU.is_equal))
                chain(nc.vector.tensor_tensor(cand[:, lo:hi, :], eq[:, lo:hi, :], rev[:].unsqueeze(1).to_broadcast([P, n, E]), ALU.mult))
                chain(nc.vector.tensor_reduce(best[:, lo:hi], cand[:, lo:hi, :], AX_X, ALU.max))
                nc.vector.tensor_tensor(one_hot[:, :, lo:hi].rearrange("p e t -> p t e"), cand[:, lo:hi, :],
                                        best[:, lo:hi].unsqueeze(2).to_broadcast([P, n, E]),
                                        ALU.is_equal).then_inc(hot_ready, 1)

            dve.wait_ge(sig_ready, 1)
            nc.vector.tensor_tensor(siluc[:], sigs[:, 0:8], c_t, ALU.mult).then_inc(silu_ready, 1)
            stats1(0, 4)
            def gate_rows_out(h):
                dve.wait_ge(mod_done, 1)
                graw = bank[6][0:B, h * D:(h + 1) * D]
                nc.vector.tensor_scalar(gsign[:], graw, 0.0, 0.5, ALU.is_ge, ALU.subtract)
                chain(nc.vector.tensor_scalar(gneg[:], graw, -2.0, None, ALU.mult))
                chain(nc.vector.scalar_tensor_tensor(out=gabs[:], in0=graw, scalar=2.0, in1=gneg[:], op0=ALU.mult,
                                                     op1=ALU.max))
                ins = nc.vector.scalar_tensor_tensor(out=grow[:, h * D:(h + 1) * D], in0=gabs[:], scalar=0.5,
                                                     in1=gsign[:], op0=ALU.max, op1=ALU.mult)
                ins.then_inc(grow_ready, 1)
                return ins

            def norm1(b):
                s = b % 2
                dve.wait_ge(rstd1_ready, min(b // 2 + 1, 3))
                if b >= 2:
                    dve.wait_ge(t1_done, b - 1)
                for t in range(TPB):
                    g = b * TPB + t
                    last = nc.vector.tensor_scalar(xn1[s][:, t * D:(t + 1) * D], x_all[:, g, :], mv1[:, g, 0:1],
                                                   rstd1[:, g:g + 1], ALU.subtract, ALU.mult)
                last.then_inc(xn1_ready, 1)

            def norm2(b):
                s = b % 2
                dve.wait_ge(rstd2_ready, b + 1)
                if b >= 2:
                    dve.wait_ge(t2_done, b - 1)
                for t in range(TPB):
                    last = nc.vector.tensor_scalar(xn2[s][:, t * D:(t + 1) * D], x1[:, b * TPB + t, :],
                                                   mv2[s][:, t, 0:1], rstd2[s][:, t:t + 1], ALU.subtract, ALU.mult)
                last.then_inc(xn2_ready, 1)

            def masked(b):
                dve.wait_ge(s_done, b + 1)
                if b >= 2:
                    dve.wait_ge(y_done, b - 1)
                nc.vector.tensor_tensor(p_t[b % 2][:], bank[3][:, 0:3 * P], decay_pow[:], ALU.mult).then_inc(p_ready, 1)

            def top_logit(b):
                dve.wait_ge(logit_done, b + 1)
                nc.vector.tensor_reduce(top[:, b * TPB:(b + 1) * TPB], bank[6][:, b * TPB * E:(b + 1) * TPB * E].rearrange(
                    "p (t e) -> p t e", t=TPB), AX_X, ALU.max).then_inc(top_ready, 1)

            def attended(b):
                s = b % 2
                dve.wait_ge(y_done, b + 1)
                dve.wait_ge(xb_ready, b + 1)
                nc.vector.tensor_tensor(x1[:, b * TPB:(b + 1) * TPB, :], bank[4][:, 0:L].rearrange("p (t d) -> p t d", t=TPB),
                                        xb[:, b * L:(b + 1) * L].rearrange("p (t d) -> p t d", t=TPB), ALU.add
                                        ).then_inc(x1_ready, 1)

            def stats2(b):
                s = b % 2
                dve.wait_ge(x1_ready, b + 1)
                for t in range(TPB):
                    last = nc.vector.bn_stats(st2[s][:, t, :], x1[:, b * TPB + t, :])
                last.then_inc(st2_step, 1)

            def moments2(b):
                s = b % 2
                dve.wait_ge(st2_step, b + 1)
                for t in range(TPB):
                    last = nc.vector.bn_aggr(mv2[s][:, t, :], st2[s][:, t, :])
                last.then_inc(mv2_ready, 1)

            def modulation_out(h):
                dve.wait_ge(mod_done, 2 + h)
                mod_t = bank[(1, 7)[h]][:, 2 * h * B:(2 * h + 2) * B].rearrange("p (k b) -> p k b", k=2)
                nc.vector.tensor_copy(shsc[:, 2 * h, :], mod_t[:, 0, :])
                nc.vector.tensor_scalar(shsc[:, 2 * h + 1, :], mod_t[:, 1, :], 1.0, None, ALU.add).then_inc(mod_ready, 1)

            gate_rows_out(0)
            modulation_out(0)
            norm1(0)
            dve.wait_ge(grow_ready, 1)
            gate_rows_out(1)
            modulation_out(1)
            norm1(1)
            dve.wait_ge(sig_ready, 2)
            chain(nc.vector.tensor_scalar(decay[:], sigs[:, 8:9], DECAY_MAX - DECAY_MIN, DECAY_MIN, ALU.mult, ALU.add))
            dve.wait_ge(const_ready, 1)
            chain(nc.vector.tensor_tensor_scan(decay_pow[:, 0:2 * P], decay[:].to_broadcast([P, 2 * P]), ident[:], 0.0,
                                               ALU.mult, ALU.add))
            chain(nc.vector.tensor_copy(decay_pow[:, 2 * P:3 * P], decay_pow[:, 0:P]))
            stats1(4, 8)
            stats1(8, NT)

            for b in range(1, B + 3):
                if b - 1 < B:
                    masked(b - 1)
                if b + 1 < B:
                    norm1(b + 1)
                if 0 <= b - 2 < B:
                    norm2(b - 2)
                if 0 <= b - 3:
                    top_logit(b - 3)
                if b - 1 < B:
                    attended(b - 1)
                    stats2(b - 1)
                    moments2(b - 1)
                if b == B + 1:
                    choose(0, NT - TPB)
            choose(NT - TPB, NT)

            dve.wait_ge(rank_done, 1)
            ranks = bank[4]
            flat = lambda a: a[:].rearrange("p e t -> p (e t)")
            chain(nc.vector.tensor_tensor_scan(flat(upto), first0[:], ranks[:, NT * E:2 * NT * E], 0.0,
                                               ALU.mult, ALU.add))
            nc.vector.tensor_tensor(flat(place), ranks[:, 0:NT * E], flat(upto), ALU.add)
            chain(nc.vector.tensor_tensor_scan(ends[:], onef[:, 0:E], upto[:, :, NT - 1], 0.0, ALU.mult, ALU.add))
            chain(nc.vector.tensor_tensor(base[:], ends[:], upto[:, :, NT - 1], ALU.subtract))
            chain(nc.vector.tensor_tensor(place[:], place[:], base[:].unsqueeze(2).to_broadcast([P, E, NT]), ALU.add))
            chain(nc.vector.tensor_tensor(place[:], place[:], one_hot[:], ALU.mult))
            with nc.allow_low_precision(reason="whole numbers below 2^24"):
                nc.vector.tensor_reduce(pos[:], place[:].rearrange("p e t -> p t e"), AX_X, ALU.add).then_inc(pos_ready, 1)

            def visits():
                chain(nc.vector.tensor_tensor(ended[:], ends[:, 0:E - 1].unsqueeze(1).to_broadcast([P, NT - 1, E - 1]),
                                              tile_end[:].unsqueeze(2).to_broadcast([P, NT - 1, E - 1]), ALU.is_le))
                chain(nc.vector.tensor_reduce(boundary[:], ended[:], AX_X, ALU.add))
                chain(nc.vector.tensor_tensor(boundary[:], boundary[:], tiles_f[:], ALU.add))
                chain(nc.vector.tensor_tensor(passed[:], boundary[:].unsqueeze(1).to_broadcast([P, NV, NT - 1]),
                                              before[:].unsqueeze(2).to_broadcast([P, NV, NT - 1]), ALU.is_le))
                chain(nc.vector.tensor_reduce(tile[:], passed[:], AX_X, ALU.add))
                nc.vector.scalar_tensor_tensor(out=expert[:, 4:NV + 4], in0=before[:], scalar=1.0, in1=tile[:],
                                               op0=ALU.add, op1=ALU.subtract)
                chain(nc.vector.tensor_scalar(tile_start[:, 2:NV + 2], tile[:], float(P), None, ALU.mult))
                nc.vector.tensor_copy(sum_at[:, 0:NV], tile_start[:, 2:NV + 2])
                nc.vector.tensor_scalar(weights_at[:], expert[:, 4:NV + 5], float(2 * F), None, ALU.mult)
                nc.vector.tensor_copy(offsets[:, :, 0, :], tile_start[:].rearrange("p (g k) -> p g k", k=RING))
                nc.vector.tensor_scalar(offsets[:, :, 1, :], expert[:].rearrange("p (g k) -> p g k", k=RING),
                                        float(FB * D), None, ALU.mult)
                chain(nc.vector.tensor_tensor(ends_row[:], ends[:, 0:E - 1], row_f[:], ALU.subtract))
                chain(nc.vector.tensor_tensor(behind[:], ends_row[:].unsqueeze(1).to_broadcast([P, NV, E - 1]),
                                              tile_start[:, 2:NV + 2].unsqueeze(2).to_broadcast([P, NV, E - 1]), ALU.is_le))
                chain(nc.vector.tensor_reduce(owner[:], behind[:], AX_X, ALU.add))
                nc.vector.tensor_tensor(mask[:], owner[:], expert[:, 4:NV + 4], ALU.is_equal).then_inc(visits_ready, 1)

            def shared_act(h):
                g = h // FB
                dve.wait_ge(shsilu_ready, h + 1)
                if g >= 2:
                    dve.wait_ge(shdown_done, g - 1)
                nc.vector.tensor_tensor(acts[g % 2][:, (h % FB) * 512:(h % FB + 1) * 512], bank[UP_BANK[h % 3]][:],
                                        sg[h % FB][:], ALU.mult).then_inc(shact_ready, 1)

            def shared_out(g):
                s = g % 2
                dve.wait_ge(shdown_done, g + 1)
                gb = gb_all[:, g * BG:(g + 1) * BG, :]
                nc.vector.tensor_tensor(
                    shg[s][:].rearrange("p (b t d) -> p b t d", b=BG, t=TPB),
                    bank[6 + s][:].rearrange("p (b t d) -> p b t d", b=BG, t=TPB),
                    gb.unsqueeze(2).to_broadcast([P, BG, TPB, D]), ALU.mult).then_inc(shg_ready, 1)
                dve.wait_ge(shg_ready, g + 1)
                nc.vector.tensor_tensor(x1[:, g * TG:(g + 1) * TG, :], x1[:, g * TG:(g + 1) * TG, :],
                                        shg[s][:].rearrange("p (t d) -> p t d", t=TG), ALU.add).then_inc(base_ready, 1)

            dve.wait_ge(gab_in[1], 16)
            shared_act(0)
            shared_act(1)
            visits()
            for g in range(G):
                if g + 1 < G:
                    shared_act(2 * g + 2)
                shared_out(g)
                if g + 1 < G:
                    shared_act(2 * g + 3)

            def act_out(v, s):
                dve.wait_ge(silu_e_ready, v + 1)
                if not isinstance(v, int) or v >= 2:
                    dve.wait_ge(down_done, v - 1)
                nc.vector.tensor_tensor(acte[s][:], bank[s][:, F:2 * F], sge[s][:], ALU.mult).then_inc(act_ready, 1)

            def load_places(g):
                _, values = nc.values_load_multi_w_load_instructions(
                    sum_at[0:1, ds(g * RING, RING)], engines=(mybir.EngineType.DVE,),
                    min_val=0, max_val=(NT - 1) * D, skip_runtime_bounds_check_because="a tile's start")
                return values

            def sum_out(v, s, place):
                dve.wait_ge(down_done, v + 1)
                if not isinstance(v, int) or v >= 1:
                    dve.wait_ge(sum_ready, v)
                nc.vector.scalar_tensor_tensor(out=routed[:, ds(place, D)], in0=bank[2 + s][:, 0:D],
                                               scalar=mask[:, ds(v, 1)], in1=routed[:, ds(place, D)],
                                               op0=ALU.mult, op1=ALU.add).then_inc(sum_ready, 1)

            def y_out(t, k, wave):
                if wave is not None:
                    dve.wait_ge(added[k], 16 * wave)
                if isinstance(t, int) and t == 0:
                    for n in range(len(CHUNKS)):
                        dve.wait_ge(rows_in[n], 16)
                dve.wait_ge(sum_ready, t + E)
                nc.vector.tensor_tensor(y[k][:], routed[:, ds(t * D, D)],
                                        rows[:, ds(t, 1), D:2 * D].rearrange("p a d -> p (a d)"),
                                        ALU.mult).then_inc(y_ready, 1)

            FIRST = E + 1
            act_out(0, 0)
            act_out(1, 1)
            dve.wait_ge(visits_ready, 1)
            dve.wait_ge(const_ready, 3)
            for v in range(2, 2 + 2 * RING):
                if (v - 2) % RING == 0:
                    sums = load_places((v - 2) // RING)
                act_out(v, v % 2)
                sum_out(v - 2, v % 2, sums[(v - 2) % RING])
                if v >= FIRST:
                    y_out(v - FIRST, (v - FIRST) % RING, None)
            for v in range(2 + 2 * RING, 2 + 3 * RING):
                if (v - 2) % RING == 0:
                    sums = load_places((v - 2) // RING)
                act_out(v, v % 2)
                sum_out(v - 2, v % 2, sums[(v - 2) % RING])
                y_out(v - FIRST, (v - FIRST) % RING, (v - FIRST) // RING or None)
            with dve.Fori(3, (NV - 2) // RING) as i:
                for k in range(RING):
                    v = i * RING + (2 + k)
                    act_out(v, k % 2)
                    if k == 0:
                        sums = load_places(i)
                    sum_out(v - 2, k % 2, sums[k])
                    y_out(i * RING + (2 + k - FIRST), (k + 1) % RING, i + (2 + k - FIRST) // RING)
            for v in range(2 + (NV - 2) // RING * RING, NV + 2):
                if v < NV:
                    act_out(v, v % 2)
                if (v - 2) % RING == 0:
                    sums = load_places((v - 2) // RING)
                sum_out(v - 2, v % 2, sums[(v - 2) % RING])
                y_out(v - FIRST, (v - FIRST) % RING, (v - FIRST) // RING)

        @block.tensor
        def _(pe):
            pe.wait_ge(mod_gate_in, 16)
            pe.wait_ge(silu_ready, 1)
            nc.tensor.matmul(bank[6][0:B, 0:2 * D], siluc[:], wmod[:, 0:2 * D], start=True, stop=True).then_inc(mod_done, 1)
            pe.wait_ge(proj_in, 16)
            nc.tensor.matmul(bank[3][:, 0:D], projs[:, 0:D], projs[:, D:2 * D], start=True, stop=True)
            nc.tensor.matmul(bank[3][:, D:2 * D], projs[:, 2 * D:3 * D], projs[:, 3 * D:4 * D], start=True,
                             stop=True).then_inc(merge_done, 1)
            pe.wait_ge(mod_in, 16)

            def modulation(n):
                for m in (n, n + 1):
                    last = nc.tensor.matmul(bank[(1, 7)[n // 2]][:, m * B:(m + 1) * B], wmod[:, (2 + m) * D:(3 + m) * D],
                                            siluc[:], start=True, stop=True)
                last.then_inc(mod_done, 1)

            modulation(0)

            def t1(b):
                pe.wait_ge(xn1_ready, b + 1)
                if b >= 1:
                    pe.wait_ge(h_ready, b)
                for t in range(TPB):
                    last = nc.tensor.transpose(bank[0][:, t * P:(t + 1) * P], xn1[b % 2][:, t * D:(t + 1) * D], ident[:, 0:P])
                last.then_inc(t1_done, 1)

            def project(b):
                s = b % 2
                pe.wait_ge(h_ready, b + 1)
                pe.wait_ge(wvog_ready, b + 1)
                if b >= 1:
                    pe.wait_ge(vo_ready, b)
                    pe.wait_ge(q_ready, b)
                for t in range(TPB):
                    last = nc.tensor.matmul(bank[2][:, t * 256:t * 256 + D + 1], h_t[s][:, t * P:(t + 1) * P],
                                            wvog[:, b * (D + 2):b * (D + 2) + D + 1], start=True, stop=True)
                last.then_inc(vo_done, 1)
                nc.tensor.matmul(bank[1][:, 0:L], a_sb[:], h_t[s][:], start=True, stop=True).then_inc(q_done, 1)

            def scores(b):
                s = b % 2
                pe.wait_ge(q_ready, b + 1)
                if b >= 1:
                    pe.wait_ge(p_ready, b)
                nc.tensor.matmul(bank[3][:, 0:L], h_t[s][:, 0:P], q_t[s][:], start=True, stop=True)
                nc.tensor.matmul(bank[3][:, L:L + P], h_t[s][:, P:L], q_t[s][:, P:L], start=True, stop=True).then_inc(s_done, 1)

            def attend(b):
                s = b % 2
                pe.wait_ge(p_ready, b + 1)
                pe.wait_ge(vo_ready, b + 1)
                if b >= 1:
                    pe.wait_ge(x1_ready, b)
                else:
                    pe.wait_ge(ga_ready, 1)
                nc.tensor.matmul(bank[4][:, 0:D], p_t[s][:, 0:P], vo[s][:, 0:D], start=True, stop=True)
                nc.tensor.matmul(bank[4][:, D:2 * D], p_t[s][:, P:2 * P], vo[s][:, 0:D], start=True, stop=False)
                nc.tensor.matmul(bank[4][:, D:2 * D], p_t[s][:, 2 * P:3 * P], vo[s][:, D:2 * D], start=False,
                                 stop=True).then_inc(y_done, 1)

            def t2(b):
                pe.wait_ge(xn2_ready, b + 1)
                if b >= 1:
                    pe.wait_ge(h2_ready, b)
                for t in range(TPB):
                    last = nc.tensor.transpose(bank[5][:, t * P:(t + 1) * P], xn2[b % 2][:, t * D:(t + 1) * D], ident[:, 0:P])
                last.then_inc(t2_done, 1)

            def router(b):
                pe.wait_ge(h2_ready, b + 1)
                if b >= 1:
                    pe.wait_ge(top_ready, b)
                if b == B - 1:
                    pe.wait_ge(hot_ready, 1)
                for g in range(b * TPB, (b + 1) * TPB):
                    last = nc.tensor.matmul(bank[6][:, g * E:(g + 1) * E], h2_all[:, g * P:(g + 1) * P], gate_w,
                                            start=True, stop=True)
                last.then_inc(logit_done, 1)
                if b >= 1:
                    pe.wait_ge(xs_ready, b)
                for t in range(TPB):
                    g = b * TPB + t
                    last = nc.tensor.transpose(bank[7][:, t * D:(t + 1) * D], h2_all[:, g * P:(g + 1) * P], ident[:, 0:P])
                last.then_inc(t3_done, 1)

            pe.wait_ge(const_ready, 1)
            def shared_up(h, u):
                g, f = h // FB, h % FB
                return nc.tensor.matmul(bank[(GATE_BANK, UP_BANK)[u][h % 3]][:],
                                        wgu[:, SH + u * F + f * P:SH + u * F + (f + 1) * P],
                                        h2_all[:, g * 512:(g + 1) * 512], start=True, stop=True)

            pe.wait_ge(grow_ready, 1)
            for b in range(2):
                last = nc.tensor.matmul(bank[4][:, b * D:(b + 1) * D], ident[0:B, b:b + 1].to_broadcast([B, P]),
                                        grow[:, 0:D], start=True, stop=True)
            last.then_inc(ga_done, 1)
            t1(0)
            modulation(2)
            pe.wait_ge(merge_ready, 1)
            pe.wait_ge(wg_ready, 1)
            for b in range(B + 3):
                if b < B and b > 0:
                    t1(b)
                if 0 <= b - 1 < B:
                    scores(b - 1)
                if b >= 3:
                    t2(b - 3)
                if b < B:
                    project(b)
                if b == B:
                    pe.wait_ge(shared_in, 32)
                    shared_up(0, 0)
                if b == B + 1:
                    shared_up(0, 1).then_inc(shgu_done, 1)
                if b == B + 2:
                    shared_up(1, 0)
                if b >= 3:
                    router(b - 3)
                if 0 <= b - 1 < B:
                    attend(b - 1)

            shared_up(1, 1).then_inc(shgu_done, 1)

            pe.wait_ge(hot_ready, 2)
            hot = one_hot[:].rearrange("p e t -> p (e t)")
            nc.tensor.matmul(bank[4][:, 0:NT * E], upto_self[:], hot, start=True, stop=True)
            nc.tensor.matmul(bank[4][:, NT * E:2 * NT * E], oneb[:], hot, start=True, stop=True).then_inc(rank_done, 1)

            def shared_half(h):
                if h >= 3:
                    pe.wait_ge(shact_ready, h - 2)
                shared_up(h, 0)
                if h == 2:
                    pe.wait_ge(pos_ready, 1)
                shared_up(h, 1).then_inc(shgu_done, 1)

            def shared_down(g):
                pe.wait_ge(shact_ready, g * FB + FB)
                if g == 1:
                    pe.wait_ge(xs_ready, B)
                if g >= 2:
                    pe.wait_ge(base_ready, g - 1)
                for t in range(TG):
                    for f in range(FB):
                        last = nc.tensor.matmul(bank[6 + g % 2][:, t * D:(t + 1) * D],
                                                acts[g % 2][:, f * 512 + t * P:f * 512 + (t + 1) * P],
                                                wdn[:, SHD + f * D:SHD + (f + 1) * D], start=(f == 0), stop=(f == FB - 1))
                last.then_inc(shdown_done, 1)

            for g in range(G):
                if g + 1 < G:
                    shared_half(2 * g + 2)
                shared_down(g)
                if g + 1 < G:
                    shared_half(2 * g + 3)

            pe.wait_ge(visits_ready, 1)
            pe.wait_ge(routed_in, 32)

            def t_rows(n):
                lo, hi = CHUNKS[n]
                pe.wait_ge(rows_in[n], 16)
                if n == 2:
                    pe.wait_ge(base_ready, G)
                if n >= 3:
                    pe.wait_ge(xr_ready, n - 2)
                for t in range(lo, hi):
                    last = nc.tensor.transpose(bank[CHUNK_BANK[n]][:, (t - lo) * P:(t - lo + 1) * P], rows[:, t, 0:D],
                                               ident[:, 0:P])
                last.then_inc(xr_done, 1)

            def gate_up(v, s, k, chunks, start):
                pe.wait_ge(w_ready, v + 1)
                pe.wait_ge(xr_ready, chunks)
                if not isinstance(v, int) or v >= 2:
                    pe.wait_ge(act_ready, v - 1)
                for n in range(2 * FB):
                    last = nc.tensor.matmul(bank[s][:, n * P:(n + 1) * P], w_now[k][:, n * P:(n + 1) * P],
                                            xs_all[:, ds(start, P)], start=True, stop=True)
                last.then_inc(gu_done, 1)

            def down(v, s, start):
                pe.wait_ge(act_ready, v + 1)
                if not isinstance(v, int) or v >= 2:
                    pe.wait_ge(sum_ready, v - 1)
                for f in range(FB):
                    last = nc.tensor.matmul(bank[2 + s][:, 0:D], acte[s][:, f * P:(f + 1) * P],
                                            wdn[:, ds(start + f * D, D)], start=(f == 0), stop=(f == FB - 1))
                last.then_inc(down_done, 1)

            def load_offsets(g):
                _, values = nc.values_load_multi_w_load_instructions(
                    offsets[0:1, ds(g, 1), :, :].rearrange("p a u k -> p (a u k)"), engines=(mybir.EngineType.PE,),
                    min_val=0, max_val=(NT - 1) * P,
                    skip_runtime_bounds_check_because="a count of at most NT - 1 or E - 1 ends")
                return (values[0:RING], [v.with_bounds(min_val=0, max_val=(E - 1) * FB * D) for v in values[RING:2 * RING]])

            row_start, down_start = load_offsets(0)
            t_rows(0)
            t_rows(1)
            for v in range(2):
                gate_up(v, v % 2, v % RING, v + 1, row_start[v + 2])
            t_rows(2)
            row_start, down_start = load_offsets(1)
            for v in range(2, 2 + RING):
                gate_up(v, v % 2, v % RING, 3 if v < 4 else 4, row_start[v - 2])
                down(v - 2, v % 2, down_start[v - 2])
                if v in (2, 3, 4):
                    t_rows(v + 1)
            with pe.Fori(1, (NV - 2) // RING) as i:
                row_start, down_start = load_offsets(i + 1)
                for k in range(RING):
                    v = i * RING + (2 + k)
                    gate_up(v, k % 2, (2 + k) % RING, len(CHUNKS), row_start[k])
                    down(v - 2, k % 2, down_start[k])
            for v in range(2 + (NV - 2) // RING * RING, NV + 2):
                if (v + 2) % RING == 0:
                    row_start, down_start = load_offsets((v + 2) // RING)
                if v < NV:
                    gate_up(v, v % 2, v % RING, len(CHUNKS), row_start[(v + 2) % RING])
                down(v - 2, v % 2, down_start[(v + 2) % RING])


def kernel(**inputs):
    import numpy as np
    import concourse.bacc as bacc
    from concourse import mybir as mb
    from concourse.bass_utils import run_bass_kernel_spmd

    a = {k: np.asarray(v) for k, v in inputs.items()}
    at, ff = "L0_attn_", "L0_ffn_"
    gates = np.concatenate([a[ff + "r_gate"], a[ff + "shared_gate"][None]])
    ups = np.concatenate([a[ff + "r_up"], a[ff + "shared_up"][None]])
    downs = np.concatenate([a[ff + "r_down"], a[ff + "shared_down"][None]])
    wmod = a["L0_wmod"]
    arrays = {
        "x": a[at + "x"],
        "proj": np.concatenate([a[at + "Wq"].T, a[at + "Wk"].T, a[at + "Wv"].T, a[at + "Wo"]], axis=1),
        "row": np.concatenate([a[at + "bo"], a[at + "bg"], a[at + "decay_param"]]),
        "c": a["L0_c"].T,
        "modin": np.concatenate([wmod[:, k * D:(k + 1) * D] for k in (2, 5, 0, 1, 3, 4)] + [ a[at + "Wg"], a[ff + "gate_w"].T], axis=1),
        "w_gu": np.concatenate([gates, ups], axis=1).transpose(2, 0, 1).reshape(D, -1),
        "w_down": downs.transpose(0, 2, 1).reshape(E + 1, FB, P, D).transpose(2, 0, 1, 3).reshape(P, -1),
    }
    arrays = {k: np.ascontiguousarray(v) for k, v in arrays.items()}
    nc = bacc.Bacc("TRN2", target_bir_lowering=False, num_devices=1)
    args = [nc.dram_tensor(k, v.shape, mb.dt.from_np(v.dtype), kind="ExternalInput").ap() for k, v in arrays.items()]
    out = nc.dram_tensor("out", (B, L, D), F32, kind="ExternalOutput").ap()
    adaln_block(nc, *args, out)
    return run_bass_kernel_spmd(nc, [arrays], core_ids=[0]).results[0]["out"]
```
